# Optimizing a Trainium2 kernel written in Bass

```python
import numpy as np
import jax
import jax.numpy as jnp

def _softmax(x, axis=-1):
    return jax.nn.softmax(x, axis=axis)

def _gelu(x):
    return jax.nn.gelu(x, approximate=True)

def _silu(x):
    return jax.nn.silu(x)

def _sigmoid(x):
    return jax.nn.sigmoid(x)

def _layernorm(x, axis=-1, eps=1e-05):
    m = jnp.mean(x, axis=axis, keepdims=True)
    v = jnp.var(x, axis=axis, keepdims=True)
    return (x - m) / jnp.sqrt(v + eps)

def _scatter_add(tgt, idx, src, axis=0):
    return tgt.at[idx].add(src)

def _segment_sum(src, seg, n):
    return jax.ops.segment_sum(src, seg, n)
kernel_name = 'mk_xattn_ffn_d1_seqx_r4_45d182'

def setup_inputs(seed: int=0):
    np.random.seed(seed)
    _w = jnp.asarray

    def _rec_inputs():
        import jax
        import jax.numpy as jnp
        _rk = jax.random.key(seed)
        x = 2.818e-05 + 1 * jax.random.normal(jax.random.fold_in(_rk, 1), (32, 128, 256), jnp.float32)
        _lenS = 128 - jax.random.randint(jax.random.fold_in(_rk, 7), (32,), 0, max(1, 128 // 4) + 1, jnp.int32)
        _lenS2 = 128 - jax.random.randint(jax.random.fold_in(_rk, 8), (32,), 0, max(1, 128 // 4) + 1, jnp.int32)
        _ctx_2048P = jax.random.normal(jax.random.fold_in(_rk, 11), (32, 16, 512), jnp.float32)
        _ctx_2048c = jax.random.dirichlet(jax.random.fold_in(_rk, 511), 0.3 * jnp.ones((16,), jnp.float32), (32, 128))
        _ctx_2048t = jnp.einsum('bsk,bkd->bsd', _ctx_2048c, _ctx_2048P)
        _ctx_2048t = _ctx_2048t * jax.lax.rsqrt(jnp.mean(jnp.square(_ctx_2048t)) + 1e-12) * 0.953939
        ctx_2048 = -0.000125008 + 0.999885 * (_ctx_2048t + 0.3 * jax.random.normal(jax.random.fold_in(_rk, 611), (32, 128, 512), jnp.float32))
        _validS = jnp.arange(128)[None, :] < _lenS[:, None]
        _validS2 = jnp.arange(128)[None, :] < _lenS2[:, None]
        _causal = jnp.tril(jnp.ones((128, 128), dtype=bool))
        mask_BxS2_fk1 = jnp.where(jnp.broadcast_to(_validS2[:, :], (32, 128)), 1.0, 0.0).astype(jnp.float32)
        return (x, ctx_2048, mask_BxS2_fk1)
    x, ctx_2048, mask_BxS2_fk1 = _rec_inputs()

    def _L0_xattn_setup():
        import jax, jax.numpy as jnp
        import numpy as np
        B, S, T = (32, 128, 128)
        SRC_SIZE, TGT_SIZE, OUT_SIZE, NUM_HEAD = (512, 256, 256, 8)
        HEAD_DIM = OUT_SIZE // NUM_HEAD
        key = jax.random.key(seed)
        ks = jax.random.split(key, 12)
        src = jax.random.normal(ks[0], (B, S, SRC_SIZE), dtype=jnp.float32)
        tgt = jax.random.normal(ks[1], (B, T, TGT_SIZE), dtype=jnp.float32)
        src_mask = (jax.random.uniform(ks[2], (B, S)) > 0.3).astype(jnp.float32)
        src_mask = src_mask.at[:, 0].set(1.0)
        tgt_mask = (jax.random.uniform(ks[3], (B, T)) > 0.3).astype(jnp.float32)
        tgt_mask = tgt_mask.at[:, 0].set(1.0)

        def lin(k, out_f, in_f):
            return jax.random.normal(k, (out_f, in_f), dtype=jnp.float32) / np.sqrt(in_f)
        W_src = lin(ks[4], 2 * OUT_SIZE, SRC_SIZE)
        b_src = jnp.zeros((2 * OUT_SIZE,), jnp.float32)
        W_tgt = lin(ks[5], OUT_SIZE, TGT_SIZE)
        b_tgt = jnp.zeros((OUT_SIZE,), jnp.float32)
        W_out = lin(ks[6], OUT_SIZE, OUT_SIZE + TGT_SIZE)
        b_out = jnp.zeros((OUT_SIZE,), jnp.float32)
        return {'src': src, 'tgt': tgt, 'src_mask': src_mask, 'tgt_mask': tgt_mask, 'W_src': W_src, 'b_src': b_src, 'W_tgt': W_tgt, 'b_tgt': b_tgt, 'W_out': W_out, 'b_out': b_out}
    _L0_xattn_all = _L0_xattn_setup()
    _L0_xattn_in = {k: v for k, v in _L0_xattn_all.items() if k in ('W_src', 'b_src', 'W_tgt', 'b_tgt', 'W_out', 'b_out')}
    del _L0_xattn_all

    def _L0_ffn_setup():
        import jax, jax.numpy as jnp
        import numpy as np
        D_IN, D_HID = (256, 1024)

        def _ternary(key, shape):
            return jax.random.randint(key, shape, -1, 2).astype(jnp.float32)

        def _tlin(x, w, s):
            return jnp.einsum('bsi,oi->bso', x, w) * s
        key = jax.random.key(seed)
        ks = jax.random.split(key, 12)
        inv = lambda fan: 1.0 / np.sqrt(fan).astype(np.float32)
        return {'x': jax.random.normal(ks[0], (4, 512, D_IN), dtype=jnp.float32), 'w1_w': _ternary(ks[1], (D_HID, D_IN)), 'w1_s': jax.random.uniform(ks[2], (D_HID,), dtype=jnp.float32) * inv(D_IN), 'w2_w': _ternary(ks[3], (D_HID, D_IN)), 'w2_s': jax.random.uniform(ks[4], (D_HID,), dtype=jnp.float32) * inv(D_IN), 'h1_w': _ternary(ks[5], (D_HID, D_HID)), 'h1_s': jax.random.uniform(ks[6], (D_HID,), dtype=jnp.float32) * inv(D_HID), 'h2_w': _ternary(ks[7], (D_HID, D_HID)), 'h2_s': jax.random.uniform(ks[8], (D_HID,), dtype=jnp.float32) * inv(D_HID), 'w3_w': _ternary(ks[9], (D_IN, D_HID)), 'w3_s': jax.random.uniform(ks[10], (D_IN,), dtype=jnp.float32) * inv(D_HID)}
    _L0_ffn_all = _L0_ffn_setup()
    _L0_ffn_in = {k: v for k, v in _L0_ffn_all.items() if k in ('w1_w', 'w1_s', 'w2_w', 'w2_s', 'h1_w', 'h1_s', 'h2_w', 'h2_s', 'w3_w', 'w3_s')}
    del _L0_ffn_all
    return {'x': x, 'ctx_2048': ctx_2048, 'mask_BxS2_fk1': mask_BxS2_fk1, 'L0_xattn_W_src': _L0_xattn_in['W_src'], 'L0_xattn_b_src': _L0_xattn_in['b_src'], 'L0_xattn_W_tgt': _L0_xattn_in['W_tgt'], 'L0_xattn_b_tgt': _L0_xattn_in['b_tgt'], 'L0_xattn_W_out': _L0_xattn_in['W_out'], 'L0_xattn_b_out': _L0_xattn_in['b_out'], 'L0_ffn_w1_w': _L0_ffn_in['w1_w'], 'L0_ffn_w1_s': _L0_ffn_in['w1_s'], 'L0_ffn_w2_w': _L0_ffn_in['w2_w'], 'L0_ffn_w2_s': _L0_ffn_in['w2_s'], 'L0_ffn_h1_w': _L0_ffn_in['h1_w'], 'L0_ffn_h1_s': _L0_ffn_in['h1_s'], 'L0_ffn_h2_w': _L0_ffn_in['h2_w'], 'L0_ffn_h2_s': _L0_ffn_in['h2_s'], 'L0_ffn_w3_w': _L0_ffn_in['w3_w'], 'L0_ffn_w3_s': _L0_ffn_in['w3_s']}

def reference(x, ctx_2048, mask_BxS2_fk1, L0_xattn_W_src, L0_xattn_b_src, L0_xattn_W_tgt, L0_xattn_b_tgt, L0_xattn_W_out, L0_xattn_b_out, L0_ffn_w1_w, L0_ffn_w1_s, L0_ffn_w2_w, L0_ffn_w2_s, L0_ffn_h1_w, L0_ffn_h1_s, L0_ffn_h2_w, L0_ffn_h2_s, L0_ffn_w3_w, L0_ffn_w3_s):
    import jax
    import jax.numpy as jnp

    def _L0_xattn_ref(src, tgt, src_mask, tgt_mask, W_src, b_src, W_tgt, b_tgt, W_out, b_out):
        import jax, jax.numpy as jnp
        import numpy as np
        B, S, T = (32, 128, 128)
        SRC_SIZE, TGT_SIZE, OUT_SIZE, NUM_HEAD = (512, 256, 256, 8)
        HEAD_DIM = OUT_SIZE // NUM_HEAD
        b, s, _ = src.shape
        t = tgt.shape[1]
        src_trans = jnp.einsum('bsf,of->bso', src, W_src) + b_src
        tgt_trans = jnp.einsum('btf,of->bto', tgt, W_tgt) + b_tgt
        src_trans = src_trans * src_mask[:, :, None]
        tgt_trans = tgt_trans * tgt_mask[:, :, None]
        src_key, src_val = jnp.split(src_trans, 2, axis=2)
        k = src_key.reshape(b, s, NUM_HEAD, HEAD_DIM)
        v = src_val.reshape(b, s, NUM_HEAD, HEAD_DIM)
        q = tgt_trans.reshape(b, t, NUM_HEAD, HEAD_DIM)
        scores = jnp.einsum('bthd,bshd->bhts', q, k) / np.sqrt(HEAD_DIM)
        scores = jnp.where(src_mask[:, None, None, :] == 0, -jnp.inf, scores)
        attn = jax.nn.softmax(scores, axis=-1)
        tgt_update = jnp.einsum('bhts,bshd->bthd', attn, v).reshape(b, t, OUT_SIZE)
        cat_tgt = jnp.concatenate([tgt, tgt_update], axis=2)
        return jnp.einsum('btf,of->bto', cat_tgt, W_out) + b_out

    def _L0_ffn_ref(x, w1_w, w1_s, w2_w, w2_s, h1_w, h1_s, h2_w, h2_s, w3_w, w3_s):
        import jax, jax.numpy as jnp
        import numpy as np
        D_IN, D_HID = (256, 1024)

        def _ternary(key, shape):
            return jax.random.randint(key, shape, -1, 2).astype(jnp.float32)

        def _tlin(x, w, s):
            return jnp.einsum('bsi,oi->bso', x, w) * s
        h = jax.nn.silu(_tlin(x, w1_w, w1_s)) * _tlin(x, w2_w, w2_s)
        h = jax.nn.gelu(_tlin(h, h1_w, h1_s), approximate=False)
        h = jax.nn.gelu(_tlin(h, h2_w, h2_s), approximate=False)
        return _tlin(h, w3_w, w3_s)
    x = x + _L0_xattn_ref(ctx_2048, _layernorm(x, axis=-1), mask_BxS2_fk1, mask_BxS2_fk1, L0_xattn_W_src, L0_xattn_b_src, L0_xattn_W_tgt, L0_xattn_b_tgt, L0_xattn_W_out, L0_xattn_b_out)
    x = x + _L0_ffn_ref(_layernorm(x, axis=-1), L0_ffn_w1_w, L0_ffn_w1_s, L0_ffn_w2_w, L0_ffn_w2_s, L0_ffn_h1_w, L0_ffn_h1_s, L0_ffn_h2_w, L0_ffn_h2_s, L0_ffn_w3_w, L0_ffn_w3_s)
    return x

_drawn_inputs = setup_inputs


def setup_inputs(seed=0):
    import zlib

    import numpy as np

    out = dict(_drawn_inputs(seed))
    spreads = {'L0_xattn_b_src': (0.0, 0.1), 'L0_xattn_b_tgt': (0.0, 0.1), 'L0_xattn_b_out': (0.0, 0.1)}
    factors = {}
    for name, (base, spread) in spreads.items():
        noise = np.random.default_rng([zlib.crc32(name.encode()), seed]).standard_normal(out[name].shape)
        drawn = base * np.exp(spread * noise) if base else spread * noise
        out[name] = jnp.asarray(drawn.astype(out[name].dtype))
    for name, factor in factors.items():
        out[name] = (out[name] * factor).astype(out[name].dtype)
    return out
```

```python
import numpy as np
import concourse.bass as bass
from concourse import mybir
from contextlib import ExitStack

F32, F32R, I32 = mybir.dt.float32, mybir.dt.float32r, mybir.dt.int32
ALU, ACT, AX = mybir.AluOpType, mybir.ActivationFunctionType, mybir.AxisListType

P = 128
B, D, DC, HID = 32, 256, 512, 1024
HEADS, DH = 8, 32
NB = 2
T = NB * P
TILES = B // NB
KD, KC, KH = D // P, DC // P, HID // P
ROWS = P // DH
SCALE = 1.0 / float(np.sqrt(DH))
EPS = 1e-5
STAGES = 3
PIECES = 2
CH = 1024
CHUNKS = 2 * KD + 2 * KH + KH * D // CH
MASKED = -3.0e38

PER = dict(
    x_loaded=16, ctx_loaded=16, mask_loaded=32,
    xn_ready=2, mask_bias_ready=1, stats1=4, veps1=1, rstd1=1, x_plus_b=2, res_ready=1,
    xt_done=1, k_done=1, q_done=1, v_done=1, xnT_ready=1, kT_ready=2, qT_ready=2, vb_ready=1, v_ready=2,
    scores_done=1, masked=2, max_ready=2, negmax_ready=2, exp_ready=2, recip=2, probs_ready=2,
    pt_done=4, ptA_ready=2, ptV_ready=2, av_done=2, upd_ready=2,
    o_done=2, x1_ready=2, stats2=4, veps2=2, rstd2=2, xn2_ready=2, x2t_done=2, x2hi_ready=2, x2_ready=2,
    gate_done=4, up_done=4, sil_ready=8, g_ready=8, mid_done=8, gelu_ready=16,
    hi_ready=12, h_ready=12, out_done=2, scaled=1, y_ready=2, stored=16,
    block_loaded=16 * 18, block_used=36,
)


def program(nc, x, ctxT, mask_row, mask_col, wsT, wvT, wtT, woT, b_cols, b_v, b_out, w1T, w2T, h1T, h2T,
            w3T, s_cols, s3, out):
    st = ExitStack()
    with st:
        def sb(name, shape, dt=F32):
            return st.enter_context(nc.sbuf_tensor(name, shape, dt))

        W1, W2 = sb("W1", [P, KD, HID], F32R), sb("W2", [P, KD, HID], F32R)
        H1, H2 = sb("H1", [P, KH, HID], F32R), sb("H2", [P, KH, HID], F32R)
        W3 = sb("W3", [P, KH, D], F32R)
        stage = [sb(f"stage{i}", [P, CH]) for i in range(STAGES)]
        WK, WV = sb("WK", [P, KC, D]), sb("WV", [P, KC, D])
        WQ, WO = sb("WQ", [P, KD, D]), sb("WO", [P, 2 * KD, D])
        bcols = sb("bcols", [P, 2 * KD])
        scols = sb("scols", [P, 4 * KH])
        bv_bc, bo_bc, s3_bc = sb("bv_bc", [P, D]), sb("bo_bc", [P, D]), sb("s3_bc", [P, D])
        ident = sb("ident", [P, P])
        neg_half = sb("neg_half", [P, NB])
        unequal, unequal_sum, most = sb("unequal", [P, CHUNKS]), sb("unequal_sum", [P, 1]), sb("most", [1, 1])
        flag = sb("flag", [1, 1], I32)
        x_in, cT = sb("x_in", [P, NB, D]), sb("cT", [P, KC, T])
        mrow, mcol, mbias = sb("mrow", [P, T]), sb("mcol", [P, NB]), sb("mbias", [P, T])
        st1, mv1 = sb("st1", [P, NB, 6]), sb("mv1", [P, NB, 2])
        ve1, rs1 = sb("ve1", [P, NB]), sb("rs1", [P, NB])
        st2, mv2 = sb("st2", [P, NB, 6]), sb("mv2", [P, NB, 2])
        ve2, rs2 = sb("ve2", [P, NB]), sb("rs2", [P, NB])
        xn, xnT = sb("xn", [P, NB, D]), sb("xnT", [P, KD, T])
        kT, qT = sb("kT", [P, KD, T]), sb("qT", [P, KD, T])
        vb, v = sb("vb", [P, NB, D]), sb("v", [P, NB, D])
        pr = [sb(f"pr{j}", [P, ROWS, KD, P]) for j in range(NB)]
        mx, nmx, den, rden = (sb(n, [P, NB, HEADS]) for n in ("mx", "nmx", "den", "rden"))
        pT, upd = sb("pT", [P, KD, ROWS * P]), sb("upd", [P, KD, P])
        x1, res, xn2 = sb("x1", [P, NB, D]), sb("res", [P, NB, D]), sb("xn2", [P, D])
        x2h, x2l = sb("x2h", [P, KD, T], F32R), sb("x2l", [P, KD, T], F32R)
        hAh, hAl = sb("hAh", [P, KH, T], F32R), sb("hAl", [P, KH, T], F32R)
        hBh, hBl = sb("hBh", [P, KH, T], F32R), sb("hBl", [P, KH, T], F32R)
        sil, g, y = sb("sil", [P, 2, T]), sb("g", [P, 2, 2, T]), sb("y", [P, NB, D])

        F = [st.enter_context(nc.psum_tensor(f"F{i}", [P, 2, T], F32)) for i in range(2)]
        G = [st.enter_context(nc.psum_tensor(f"G{i}", [P, 2 * T], F32)) for i in range(2)]
        S = st.enter_context(nc.psum_tensor("S", [P, ROWS, NB, KD, P], F32))

        def sem(name):
            return st.enter_context(nc.semaphore(name))

        x_loaded = sem("x_loaded")
        ctx_loaded = sem("ctx_loaded")
        mask_loaded = sem("mask_loaded")
        xn_ready = sem("xn_ready")
        mask_bias_ready = sem("mask_bias_ready")
        stats1 = sem("stats1")
        veps1 = sem("veps1")
        rstd1 = sem("rstd1")
        x_plus_b = sem("x_plus_b")
        res_ready = sem("res_ready")
        xt_done = sem("xt_done")
        k_done = sem("k_done")
        q_done = sem("q_done")
        v_done = sem("v_done")
        xnT_ready = sem("xnT_ready")
        kT_ready = sem("kT_ready")
        qT_ready = sem("qT_ready")
        vb_ready = sem("vb_ready")
        v_ready = sem("v_ready")
        scores_done = sem("scores_done")
        masked = sem("masked")
        max_ready = sem("max_ready")
        negmax_ready = sem("negmax_ready")
        exp_ready = sem("exp_ready")
        recip = sem("recip")
        probs_ready = sem("probs_ready")
        pt_done = sem("pt_done")
        ptA_ready = sem("ptA_ready")
        ptV_ready = sem("ptV_ready")
        av_done = sem("av_done")
        upd_ready = sem("upd_ready")
        o_done = sem("o_done")
        x1_ready = sem("x1_ready")
        stats2 = sem("stats2")
        veps2 = sem("veps2")
        rstd2 = sem("rstd2")
        xn2_ready = sem("xn2_ready")
        x2t_done = sem("x2t_done")
        x2hi_ready = sem("x2hi_ready")
        x2_ready = sem("x2_ready")
        gate_done = sem("gate_done")
        up_done = sem("up_done")
        sil_ready = sem("sil_ready")
        g_ready = sem("g_ready")
        mid_done = sem("mid_done")
        gelu_ready = sem("gelu_ready")
        hi_ready = sem("hi_ready")
        h_ready = sem("h_ready")
        out_done = sem("out_done")
        y_ready = sem("y_ready")
        block_used = sem("block_used")
        scaled = [sem(f"scaled{j}") for j in range(2)]
        stored = [sem(f"stored{j}") for j in range(2)]
        block_loaded = [sem(f"block_loaded{j}") for j in range(2)]
        consts_ready = sem("consts_ready")
        attn_w_loaded = sem("attn_w_loaded")
        small_loaded = sem("small_loaded")
        chunk_cast = sem("chunk_cast")
        chunk_looked = sem("chunk_looked")
        counted = sem("counted")
        low_summed = sem("low_summed")
        flag_ready = sem("flag_ready")
        stats_seen = sem("stats_seen")
        chunk_loaded = [sem(f"chunk_loaded{i}") for i in range(STAGES)]
        def at(name, tile, k):
            value = tile * PER[name] + k
            return max(value, 0) if isinstance(value, int) else value

        chunks = ([(w1T, W1, k) for k in range(KD)] + [(w2T, W2, k) for k in range(KD)]
                  + [(h1T, H1, k) for k in range(KH)] + [(h2T, H2, k) for k in range(KH)]
                  + [(w3T, W3, 4 * k) for k in range(KH * D // CH)])
        assert len(chunks) == CHUNKS
        block = st.enter_context(nc.Block())

        @block.sync
        def _(sp):
            def load_tile(a):
                sp.wait_ge(xn_ready, at("xn_ready", a - 1, 2))
                sp.wait_ge(x_plus_b, at("x_plus_b", a - 1, 2))
                sp.dma_start(x_in[:], x[bass.ds(a, 1)].rearrange("o p n -> (o p) n")).then_inc(x_loaded, 16)
                sp.wait_ge(k_done, at("k_done", a - 1, 1))
                sp.wait_ge(v_done, at("v_done", a - 1, 1))
                sp.dma_start(cT[:], ctxT[bass.ds(a, 1)].rearrange("o p n -> (o p) n")).then_inc(ctx_loaded, 16)
                sp.wait_ge(kT_ready, at("kT_ready", a - 1, 2))
                sp.wait_ge(qT_ready, at("qT_ready", a - 1, 2))
                sp.wait_ge(mask_bias_ready, at("mask_bias_ready", a - 1, 1))
                sp.dma_start(mrow[:], mask_row[bass.ds(a, 1)].broadcast_to([P, T])).then_inc(mask_loaded, 16)
                sp.wait_ge(v_ready, at("v_ready", a - 1, 2))
                sp.dma_start(mcol[:], mask_col[bass.ds(a, 1)].rearrange("o p n -> (o p) n")).then_inc(mask_loaded, 16)

            def raw_block(f, n, src):
                sp.wait_ge(block_used, at("block_used", f, max(n - 1, 0)))
                dst = stage[n % 2][:].rearrange("p (k m) -> p k m", m=src.shape[2])[:, 0:src.shape[1], :]
                sp.dma_start(dst, src).then_inc(block_loaded[n % 2], 16)

            def tile(f, a, general):
                if general:
                    for n in range(2 * KH):
                        src, p = (w1T, w2T)[n // 2 % 2], 2 * (n // 4) + n % 2
                        raw_block(f, n, src[:, :, p * P:(p + 1) * P])
                if a is not None:
                    load_tile(a)
                if general:
                    for m in range(KH):
                        raw_block(f, 16 + m, h1T[:, :, m * P:(m + 1) * P])
                    for m in range(KH):
                        raw_block(f, 24 + m, h2T[:, :, m * P:(m + 1) * P])
                    for n in range(2 * NB):
                        raw_block(f, 32 + n, w3T[:, 4 * (n % 2):4 * (n % 2) + 4, :])
                for j in range(NB):
                    sp.wait_ge(y_ready, at("y_ready", f, j + 1))
                    sp.dma_start(out[bass.ds(f * NB + j, 1)].rearrange("o p n -> (o p) n"), y[:, j, :]).then_inc(stored[j], 16)

            def tiles(general):
                tile(0, 2, general)
                with sp.Fori(1, TILES - 2) as i:
                    tile(i, i + 2, general)
                tile(TILES - 2, None, general)
                tile(TILES - 1, None, general)

            sp.dma_start(bcols[:], b_cols).then_inc(small_loaded, 16)
            load_tile(0)
            for dst, src in ((WK, wsT), (WV, wvT), (WQ, wtT), (WO, woT)):
                sp.dma_start(dst[:], src).then_inc(attn_w_loaded, 16)
            for dst, src in ((scols, s_cols), (bv_bc, b_v.broadcast_to([P, D])),
                             (bo_bc, b_out.broadcast_to([P, D])), (s3_bc, s3.broadcast_to([P, D]))):
                sp.dma_start(dst[:], src).then_inc(small_loaded, 16)
            for n, (src, _, k) in enumerate(chunks):
                if n >= STAGES:
                    sp.wait_ge(chunk_looked, n - STAGES + 1)
                w = CH // src.shape[2]
                sp.dma_start(stage[n % STAGES][:].rearrange("p (k m) -> p k m", k=w), src[:, k:k + w, :])\
                    .then_inc(chunk_loaded[n % STAGES], 16)
            load_tile(1)
            sp.wait_ge(flag_ready, 1)
            has_low_bits = sp.value_load(flag[0:1, 0:1], min_val=0, max_val=1)
            with sp.If(has_low_bits):
                tiles(True)
            with sp.Else():
                tiles(False)
            for j in range(NB):
                sp.wait_ge(stored[j], at("stored", TILES, 0))

        @block.tensor
        def _(pe):
            mm = nc.tensor.matmul

            def transposes_x(a):
                pe.wait_ge(xn_ready, at("xn_ready", a, 2))
                pe.wait_ge(x1_ready, at("x1_ready", a - 1, 2))
                for j in range(NB):
                    for c in range(KD):
                        ins = nc.tensor.transpose(G[0][:, c * T + j * P:c * T + (j + 1) * P],
                                                  xn[:, j, c * P:(c + 1) * P], ident[:])
                ins.then_inc(xt_done, 1)

            def project_k(a):
                pe.wait_ge(ctx_loaded, at("ctx_loaded", a, 16))
                pe.wait_ge(x2_ready, at("x2_ready", a - 1, 2))
                for c in range(KD):
                    for k in range(KC):
                        ins = mm(G[1][:, c * T:(c + 1) * T], WK[:, k, c * P:(c + 1) * P], cT[:, k, :],
                                 start=k == 0, stop=k == KC - 1)
                ins.then_inc(k_done, 1)

            def project_q(a):
                pe.wait_ge(xnT_ready, at("xnT_ready", a, 1))
                for c in range(KD):
                    for k in range(KD):
                        ins = mm(G[0][:, c * T:(c + 1) * T], WQ[:, k, c * P:(c + 1) * P], xnT[:, k, :],
                                 start=k == 0, stop=k == KD - 1)
                ins.then_inc(q_done, 1)

            def project_v(a):
                pe.wait_ge(kT_ready, at("kT_ready", a, 2))
                for j in range(NB):
                    for k in range(KC):
                        ins = mm(G[1][:, j * D:(j + 1) * D], cT[:, k, j * P:(j + 1) * P], WV[:, k, :],
                                 start=k == 0, stop=k == KC - 1)
                ins.then_inc(v_done, 1)

            def scores(a):
                pe.wait_ge(kT_ready, at("kT_ready", a, 2))
                pe.wait_ge(qT_ready, at("qT_ready", a, 2))
                pe.wait_ge(masked, at("masked", a - 1, 2))
                for j in range(NB):
                    for c in range(KD):
                        for r in range(ROWS):
                            rows = slice(r * DH, (r + 1) * DH)
                            ins = mm(S[:, r, j, c, :], qT[rows, c, j * P:(j + 1) * P],
                                     kT[rows, c, j * P:(j + 1) * P], start=True, stop=True)
                ins.then_inc(scores_done, 1)

            def transpose_p(a, j):
                pe.wait_ge(probs_ready, at("probs_ready", a, j + 1))
                if j == 0:
                    pe.wait_ge(qT_ready, at("qT_ready", a, 2))
                    pe.wait_ge(vb_ready, at("vb_ready", a, 1))
                else:
                    pe.wait_ge(upd_ready, at("upd_ready", a, 1))
                    pe.wait_ge(ptV_ready, at("ptV_ready", a, 1))
                for c in range(KD):
                    for r in range(ROWS):
                        ins = nc.tensor.transpose(G[c][:, r * P:(r + 1) * P], pr[j][:, r, c, :], ident[:])
                    ins.then_inc(pt_done, 1)

            def attend(a, j):
                pe.wait_ge(v_ready, at("v_ready", a, 2))
                pe.wait_ge(ptA_ready, at("ptA_ready", a, j + 1))
                for c in range(KD):
                    if c == 1:
                        pe.wait_ge(ptV_ready, at("ptV_ready", a, j + 1))
                    for r in range(ROWS):
                        h = c * ROWS + r
                        ins = mm(G[0][r * DH:(r + 1) * DH, c * P:(c + 1) * P], v[:, j, h * DH:(h + 1) * DH],
                                 pT[:, c, r * P:(r + 1) * P], start=True, stop=True)
                ins.then_inc(av_done, 1)

            def out_proj(a, j):
                bank = G[1] if j == 0 else G[0]
                if j == 0:
                    pe.wait_ge(ptV_ready, at("ptV_ready", a, 2))
                pe.wait_ge(upd_ready, at("upd_ready", a, j + 1))
                for k in range(2 * KD):
                    lhsT = xnT[:, k, j * P:(j + 1) * P] if k < KD else upd[:, k - KD, :]
                    ins = mm(bank[:, 0:D], lhsT, WO[:, k, :], start=k == 0, stop=k == 2 * KD - 1)
                ins.then_inc(o_done, 1)

            def transpose_x2(a, j):
                pe.wait_ge(xn2_ready, at("xn2_ready", a, j + 1))
                if j == 0:
                    pe.wait_ge(x1_ready, at("x1_ready", a, 1))
                else:
                    pe.wait_ge(x2_ready, at("x2_ready", a, 1))
                for c in range(KD):
                    ins = nc.tensor.transpose(G[1][:, c * P:(c + 1) * P], xn2[:, c * P:(c + 1) * P], ident[:])
                ins.then_inc(x2t_done, 1)

            def ffn_group(bank, W, cols, parts, general, f, n, ready=None):
                kk = W.shape[1]
                if general:
                    pe.wait_ge(block_loaded[n % 2], at("block_loaded", f, 16 * (n // 2 + 1)))
                    raw = stage[n % 2][:].rearrange("p (k m) -> p k m", m=P)
                for k in range(kk):
                    if ready is not None:
                        ready(k)
                    for q, part in enumerate(parts):
                        first, last = k == 0 and q == 0, k == kk - 1 and q == 1
                        if general:
                            ins = mm(bank, raw[:, k, :], part[:, k, :].bitcast(F32), start=first, stop=last)
                        else:
                            ins = mm(bank, W[:, k, cols], part[:, k, :], start=first, stop=last)
                if general:
                    ins.then_inc(block_used, 1)
                    ins = pe.nop()
                return ins

            def gate_up(f, q, general):
                pe.wait_ge(x2_ready, at("x2_ready", f, 2))
                if q == 0:
                    pe.wait_ge(scaled[0], at("scaled", f - 1, 1))
                else:
                    pe.wait_ge(sil_ready, at("sil_ready", f, 2 * q))
                for h in range(2):
                    cols = slice((2 * q + h) * P, (2 * q + h + 1) * P)
                    ins = ffn_group(F[0][:, h, :], W1, cols, (x2h, x2l), general, f, 4 * q + h)
                ins.then_inc(gate_done, 1)
                if q == 0:
                    pe.wait_ge(scaled[1], at("scaled", f - 1, 1))
                else:
                    pe.wait_ge(g_ready, at("g_ready", f, 2 * q))
                for h in range(2):
                    cols = slice((2 * q + h) * P, (2 * q + h + 1) * P)
                    ins = ffn_group(F[1][:, h, :], W2, cols, (x2h, x2l), general, f, 4 * q + 2 + h)
                ins.then_inc(up_done, 1)

            def middle(f, q, general):
                W, parts = (H1, (hAh, hAl)) if q < 8 else (H2, (hBh, hBl))
                if q == 4:
                    pe.wait_ge(sil_ready, at("sil_ready", f, KH))
                elif q == 5:
                    pe.wait_ge(g_ready, at("g_ready", f, KH))
                else:
                    pe.wait_ge(gelu_ready, at("gelu_ready", f, 2 * (q - 5)))
                for m in (2 * (q % 4), 2 * (q % 4) + 1):
                    def ready(k):
                        if m == 0 and k % 2 == 0:
                            pe.wait_ge(h_ready, at("h_ready", f, q + k // 2 + 1 - 4))

                    ins = ffn_group(F[q % 2][:, m % 2, :], W, slice(m * P, (m + 1) * P), parts, general, f,
                                    2 * KH + (q // 4 - 1) * KH + m, ready)
                ins.then_inc(mid_done, 1)

            def ffn_out(f, j, general):
                pe.wait_ge(h_ready, at("h_ready", f, 12))
                pe.wait_ge(gelu_ready, at("gelu_ready", f, 14 + 2 * j))
                for half in range(2):
                    if general:
                        pe.wait_ge(block_loaded[half], at("block_loaded", f, 16 * (KH * 2 + j + 1)))
                        raw = stage[half][:].rearrange("p (k m) -> p k m", m=D)
                    for k in range(4 * half, 4 * half + 4):
                        for q, part in enumerate((hAh, hAl)):
                            first, last = k == 0 and q == 0, k == KH - 1 and q == 1
                            lhsT = part[:, k, j * P:(j + 1) * P]
                            if general:
                                ins = mm(F[j][:, 0, :], lhsT.bitcast(F32), raw[:, k - 4 * half, :], start=first, stop=last)
                            else:
                                ins = mm(F[j][:, 0, :], lhsT, W3[:, k, :], start=first, stop=last)
                    if general:
                        ins.then_inc(block_used, 1)
                        ins = pe.nop()
                ins.then_inc(out_done, 1)

            def tile(f, a, general):
                attn, ffn = a is not None, f is not None
                for q in range(4):
                    if ffn:
                        gate_up(f, q, general)
                    if attn and q == 0:
                        transposes_x(a)
                        project_k(a)
                        project_q(a)
                    if attn and q == 1:
                        scores(a)
                if attn:
                    project_v(a)
                for q in range(4, 12):
                    if attn and q == 5:
                        transpose_p(a, 0)
                    if attn and q == 6:
                        attend(a, 0)
                    if attn and q == 7:
                        transpose_p(a, 1)
                    if attn and q == 8:
                        attend(a, 1)
                        out_proj(a, 0)
                    if attn and q == 10:
                        transpose_x2(a, 0)
                    if ffn:
                        middle(f, q, general)
                if attn:
                    out_proj(a, 1)
                if ffn:
                    ffn_out(f, 0, general)
                if attn:
                    transpose_x2(a, 1)
                if ffn:
                    ffn_out(f, 1, general)

            def tiles(general):
                tile(0, 1, general)
                with pe.Fori(1, TILES - 1) as i:
                    tile(i, i + 1, general)
                tile(TILES - 1, None, general)

            pe.wait_ge(consts_ready, 3)
            pe.wait_ge(attn_w_loaded, 64)
            tile(None, 0, False)
            pe.wait_ge(flag_ready, 1)
            has_low_bits = pe.value_load(flag[0:1, 0:1], min_val=0, max_val=1)
            with pe.If(has_low_bits):
                tiles(True)
            with pe.Else():
                tiles(False)

        @block.scalar
        def _(act):
            fn = nc.scalar.activation

            def silu(f, q):
                act.wait_ge(gate_done, at("gate_done", f, q + 1))
                for p in (2 * q, 2 * q + 1):
                    act.wait_ge(g_ready, at("g_ready", f, max(p - 1, 0)))
                    fn(sil[:, p % 2, :], F[0][:, p % 2, :], ACT.Silu, scale=scols[:, p:p + 1]).then_inc(sil_ready, 1)

            def gelu(f, q):
                act.wait_ge(mid_done, at("mid_done", f, q - 3))
                act.wait_ge(h_ready, at("h_ready", f, q - 1))
                for m in (0, 1):
                    col = KH + 2 * q + m
                    fn(g[:, q % 2, m, :], F[q % 2][:, m, :], ACT.Gelu, scale=scols[:, col:col + 1]).then_inc(gelu_ready, 1)

            def copy_xnT(a):
                act.wait_ge(xt_done, at("xt_done", a, 1))
                act.wait_ge(o_done, at("o_done", a - 1, 2))
                fn(xnT[:].rearrange("p c t -> p (c t)"), G[0][:], ACT.Copy).then_inc(xnT_ready, 1)

            def exps(a, j):
                act.wait_ge(negmax_ready, at("negmax_ready", a, j + 1))
                for r in range(ROWS):
                    for c in range(KD):
                        h = r * KD + c
                        ins = fn(pr[j][:, r, c, :], pr[j][:, r, c, :], ACT.Exp, bias=nmx[:, j, h:h + 1],
                                 scale=SCALE, accum_out=den[:, j, h:h + 1])
                ins.then_inc(exp_ready, 1)

            def scale_v(a):
                act.wait_ge(vb_ready, at("vb_ready", a, 1))
                act.wait_ge(mask_loaded, at("mask_loaded", a, 32))
                act.wait_ge(av_done, at("av_done", a - 1, 2))
                for j in range(NB):
                    fn(v[:, j, :], vb[:, j, :], ACT.Copy, scale=mcol[:, j:j + 1]).then_inc(v_ready, 1)

            def copy_pT(a, j):
                act.wait_ge(pt_done, at("pt_done", a, 2 * j + 1))
                act.wait_ge(av_done, at("av_done", a, j))
                fn(pT[:, 0, :], G[0][:], ACT.Copy).then_inc(ptA_ready, 1)

            def copy_upd(a, j):
                act.wait_ge(av_done, at("av_done", a, j + 1))
                act.wait_ge(o_done, at("o_done", a, j))
                fn(upd[:].rearrange("p c t -> p (c t)"), G[0][:, 0:KD * P], ACT.Copy).then_inc(upd_ready, 1)

            def x2_hi(a, j):
                act.wait_ge(x2t_done, at("x2t_done", a, j + 1))
                act.wait_ge(up_done, at("up_done", a - 1, 4))
                fn(x2h[:, :, j * P:(j + 1) * P], G[1][:, 0:KD * P].rearrange("p (c t) -> p c t", c=KD), ACT.Copy).then_inc(x2hi_ready, 1)

            def tile(f, a):
                attn, ffn = a is not None, f is not None
                for q in range(4):
                    if ffn:
                        silu(f, q)
                    if attn and q == 0:
                        copy_xnT(a)
                    if not ffn:
                        for n in range(PIECES * q, PIECES * (q + 1)):
                            cast(n)
                if attn:
                    exps(a, 0)
                    exps(a, 1)
                    scale_v(a)
                for q in range(4, 12):
                    if attn and q == 5:
                        copy_pT(a, 0)
                    if attn and q == 6:
                        copy_upd(a, 0)
                    if attn and q == 7:
                        copy_pT(a, 1)
                    if attn and q == 8:
                        copy_upd(a, 1)
                    if attn and q == 10:
                        x2_hi(a, 0)
                    if ffn:
                        gelu(f, q)
                if attn:
                    x2_hi(a, 1)

            def cast(n):
                _, W, k = chunks[n]
                w = CH // W.shape[2]
                act.wait_ge(chunk_loaded[n % STAGES], 16 * (n // STAGES + 1))
                fn(W[:, k:k + w, :], stage[n % STAGES][:].rearrange("p (k m) -> p k m", k=w), ACT.Copy)\
                    .then_inc(chunk_cast, 1)

            act.wait_ge(small_loaded, 80)
            tile(None, 0)
            for n in range(4 * PIECES, CHUNKS):
                cast(n)
            tile(0, 1)
            with act.Fori(1, TILES - 1) as i:
                tile(i, i + 1)
            tile(TILES - 1, None)

        @block.vector
        def _(dve):
            V = nc.vector

            def keep_residual(f):
                dve.wait_ge(x1_ready, at("x1_ready", f, 2))
                dve.wait_ge(y_ready, at("y_ready", f - 1, 2))
                V.tensor_copy(res[:], x1[:]).then_inc(res_ready, 1)

            def ln1_stats(a):
                dve.wait_ge(x_loaded, at("x_loaded", a, 16))
                for j in range(NB):
                    V.bn_stats(st1[:, j, :], x_in[:, j, :]).then_inc(stats1, 1)
                dve.wait_ge(stats1, at("stats1", a, 2))
                dve.sem_inc(stats_seen, 1)
                for j in range(NB):
                    V.bn_aggr(mv1[:, j, :], st1[:, j, :]).then_inc(stats1, 1)
                dve.wait_ge(stats1, at("stats1", a, 4))
                V.tensor_scalar_add(ve1[:], mv1[:, :, 1], EPS).then_inc(veps1, 1)

            def mask_bias(a):
                dve.wait_ge(mask_loaded, at("mask_loaded", a, 32))
                V.tensor_scalar(mbias[:], mrow[:], 0.0, MASKED, ALU.is_equal, ALU.mult).then_inc(mask_bias_ready, 1)

            def ln1_apply(a):
                dve.wait_ge(rstd1, at("rstd1", a, 1))
                dve.wait_ge(xt_done, at("xt_done", a - 1, 1))
                for j in range(NB):
                    V.tensor_scalar(xn[:, j, :], x_in[:, j, :], mv1[:, j, 0:1], rs1[:, j:j + 1],
                                        ALU.subtract, ALU.mult).then_inc(xn_ready, 1)

            def bias_mask_k(a):
                dve.wait_ge(k_done, at("k_done", a, 1))
                dve.wait_ge(mask_loaded, at("mask_loaded", a, 32))
                dve.wait_ge(scores_done, at("scores_done", a - 1, 1))
                for c in range(KD):
                    V.scalar_tensor_tensor(kT[:, c, :], G[1][:, c * T:(c + 1) * T], bcols[:, c:c + 1],
                                           mrow[:], ALU.add, ALU.mult).then_inc(kT_ready, 1)

            def bias_mask_q(a):
                dve.wait_ge(q_done, at("q_done", a, 1))
                dve.wait_ge(mask_loaded, at("mask_loaded", a, 32))
                dve.wait_ge(scores_done, at("scores_done", a - 1, 1))
                for c in range(KD):
                    V.scalar_tensor_tensor(qT[:, c, :], G[0][:, c * T:(c + 1) * T], bcols[:, KD + c:KD + c + 1],
                                           mrow[:], ALU.add, ALU.mult).then_inc(qT_ready, 1)

            def bias_v(a):
                dve.wait_ge(v_done, at("v_done", a, 1))
                dve.wait_ge(v_ready, at("v_ready", a - 1, 2))
                V.tensor_tensor(vb[:], G[1][:].rearrange("p (j n) -> p j n", j=NB),
                                    bv_bc[:].unsqueeze(1).broadcast_to([P, NB, D]), ALU.add).then_inc(vb_ready, 1)

            def mask_scores(a, j):
                dve.wait_ge(scores_done, at("scores_done", a, 1))
                dve.wait_ge(pt_done, at("pt_done", a - 1, 2 * j + 2))
                dve.wait_ge(mask_bias_ready, at("mask_bias_ready", a, 1))
                bias = mbias[:, j * P:(j + 1) * P].unsqueeze(1).unsqueeze(1).broadcast_to([P, ROWS, KD, P])
                V.tensor_tensor(pr[j][:], S[:, :, j, :, :], bias, ALU.add).then_inc(masked, 1)

            def row_max(a, j):
                dve.wait_ge(masked, at("masked", a, j + 1))
                V.tensor_reduce(mx[:, j, :], pr[j][:].rearrange("p r c s -> p (r c) s"), AX.X, ALU.max).then_inc(max_ready, 1)
                dve.wait_ge(max_ready, at("max_ready", a, j + 1))
                dve.wait_ge(exp_ready, at("exp_ready", a - 1, j + 1))
                V.tensor_scalar_mul(nmx[:, j, :], mx[:, j, :], -SCALE).then_inc(negmax_ready, 1)

            def normalise(a, j):
                dve.wait_ge(exp_ready, at("exp_ready", a, j + 1))
                V.reciprocal(rden[:, j, :], den[:, j, :]).then_inc(recip, 1)
                dve.wait_ge(recip, at("recip", a, j + 1))
                p8 = pr[j][:].rearrange("p r c s -> p (r c) s")
                V.tensor_tensor(p8, p8, rden[:, j, :].unsqueeze(2).broadcast_to([P, HEADS, P]), ALU.mult).then_inc(probs_ready, 1)

            def copy_pT(a, j):
                dve.wait_ge(pt_done, at("pt_done", a, 2 * j + 2))
                dve.wait_ge(av_done, at("av_done", a, j))
                V.tensor_copy(pT[:, 1, :], G[1][:]).then_inc(ptV_ready, 1)

            def residual_ln2_stats(a, j):
                bank = G[1] if j == 0 else G[0]
                dve.wait_ge(o_done, at("o_done", a, j + 1))
                dve.wait_ge(x_plus_b, at("x_plus_b", a, j + 1))
                V.tensor_tensor(x1[:, j, :], bank[:, 0:D], x1[:, j, :], ALU.add).then_inc(x1_ready, 1)
                dve.wait_ge(x1_ready, at("x1_ready", a, j + 1))
                V.bn_stats(st2[:, j, :], x1[:, j, :]).then_inc(stats2, 1)
                dve.wait_ge(stats2, at("stats2", a, 2 * j + 1))
                dve.sem_inc(stats_seen, 1)
                V.bn_aggr(mv2[:, j, :], st2[:, j, :]).then_inc(stats2, 1)
                dve.wait_ge(stats2, at("stats2", a, 2 * j + 2))
                V.tensor_scalar_add(ve2[:, j:j + 1], mv2[:, j, 1:2], EPS).then_inc(veps2, 1)

            def ln2_apply(a, j):
                dve.wait_ge(rstd2, at("rstd2", a, j + 1))
                dve.wait_ge(x2t_done, at("x2t_done", a, j))
                V.tensor_scalar(xn2[:], x1[:, j, :], mv2[:, j, 0:1], rs2[:, j:j + 1],
                                    ALU.subtract, ALU.mult).then_inc(xn2_ready, 1)

            def x2_lo(a, j):
                dve.wait_ge(x2hi_ready, at("x2hi_ready", a, j + 1))
                dve.wait_ge(up_done, at("up_done", a - 1, 4))
                part = slice(j * P, (j + 1) * P)
                V.tensor_tensor(x2l[:, :, part], G[1][:, 0:KD * P].rearrange("p (c t) -> p c t", c=KD),
                                    x2h[:, :, part].bitcast(F32), ALU.subtract).then_inc(x2_ready, 1)

            def gate_times_up(f, q):
                dve.wait_ge(up_done, at("up_done", f, q + 1))
                dve.wait_ge(h_ready, at("h_ready", f, max(q - 1, 0)))
                for p in (2 * q, 2 * q + 1):
                    dve.wait_ge(sil_ready, at("sil_ready", f, p + 1))
                    V.scalar_tensor_tensor(g[:, q % 2, p % 2, :], F[1][:, p % 2, :], scols[:, KH + p:KH + p + 1],
                                               sil[:, p % 2, :], ALU.mult, ALU.mult).then_inc(g_ready, 1)

            def split(f, q):
                hi, lo = ((hAh, hAl), (hBh, hBl), (hAh, hAl))[q // 4]
                pair = slice(2 * (q % 4), 2 * (q % 4) + 2)
                if q < 4:
                    dve.wait_ge(g_ready, at("g_ready", f, 2 * q + 2))
                    dve.wait_ge(out_done, at("out_done", f - 1, 2))
                elif q < 8:
                    dve.wait_ge(gelu_ready, at("gelu_ready", f, 2 * (q - 4) + 2))
                    dve.wait_ge(mid_done, at("mid_done", f - 1, 8))
                else:
                    dve.wait_ge(gelu_ready, at("gelu_ready", f, 2 * (q - 4) + 2))
                    dve.wait_ge(mid_done, at("mid_done", f, 4))
                V.tensor_copy(hi[:, pair, :], g[:, q % 2, :, :]).then_inc(hi_ready, 1)
                dve.wait_ge(hi_ready, at("hi_ready", f, q + 1))
                V.tensor_tensor(lo[:, pair, :], g[:, q % 2, :, :], hi[:, pair, :].bitcast(F32), ALU.subtract).then_inc(h_ready, 1)

            def scale_and_add(f, j):
                dve.wait_ge(out_done, at("out_done", f, j + 1))
                dve.wait_ge(stored[j], at("stored", f - 1, 16))
                V.tensor_tensor(y[:, j, :], F[j][:, 0, :], s3_bc[:], ALU.mult).then_inc(scaled[j], 1)
                dve.wait_ge(scaled[j], at("scaled", f, 1))
                V.tensor_tensor(y[:, j, :], y[:, j, :], res[:, j, :], ALU.add).then_inc(y_ready, 1)

            def tile(f, a):
                attn, ffn = a is not None, f is not None
                if ffn:
                    keep_residual(f)
                if attn:
                    ln1_stats(a)
                    mask_bias(a)
                    ln1_apply(a)
                for q in range(4):
                    if ffn:
                        gate_times_up(f, q)
                        split(f, q)
                    if attn and q == 0:
                        bias_mask_k(a)
                        bias_mask_q(a)
                    if not ffn:
                        for n in range(PIECES * q, PIECES * (q + 1)):
                            look(n)
                    if attn and q == 1:
                        mask_scores(a, 0)
                        row_max(a, 0)
                        mask_scores(a, 1)
                if attn:
                    row_max(a, 1)
                    bias_v(a)
                for q in range(4, 12):
                    if attn and q == 4:
                        normalise(a, 0)
                    if attn and q == 5:
                        copy_pT(a, 0)
                        normalise(a, 1)
                    if attn and q == 7:
                        copy_pT(a, 1)
                    if attn and q == 8:
                        residual_ln2_stats(a, 0)
                        ln2_apply(a, 0)
                    if attn and q == 10:
                        x2_lo(a, 0)
                    if ffn:
                        split(f, q)
                if attn:
                    residual_ln2_stats(a, 1)
                    ln2_apply(a, 1)
                if ffn:
                    scale_and_add(f, 0)
                if attn:
                    x2_lo(a, 1)
                if ffn:
                    scale_and_add(f, 1)

            def look(n):
                _, W, k = chunks[n]
                w = CH // W.shape[2]
                raw = stage[n % STAGES][:].rearrange("p (k m) -> p k m", k=w)
                dve.wait_ge(chunk_cast, n + 1)
                V.scalar_tensor_tensor(raw, raw, 1.0, W[:, k:k + w, :].bitcast(F32), ALU.mult, ALU.not_equal,
                                       accum_out=unequal[:, n:n + 1]).then_inc(chunk_looked, 1)

            dve.wait_ge(small_loaded, 80)
            tile(None, 0)
            for n in range(4 * PIECES, CHUNKS):
                look(n)
            dve.wait_ge(chunk_looked, CHUNKS)
            V.tensor_reduce(unequal_sum[:], unequal[:], AX.X, ALU.max).then_inc(counted, 1)
            dve.wait_ge(low_summed, 1)
            V.tensor_scalar_min(flag[:], most[:], 1.0).then_inc(flag_ready, 1)
            tile(0, 1)
            with dve.Fori(1, TILES - 1) as i:
                tile(i, i + 1)
            tile(TILES - 1, None)

        @block.gpsimd
        def _(pool):
            Gp = nc.gpsimd

            def inverse_std1(a):
                pool.wait_ge(veps1, at("veps1", a, 1))
                Gp.tensor_tensor(rs1[:], ve1[:], neg_half[:], ALU.pow).then_inc(rstd1, 1)

            def add_bias(a):
                pool.wait_ge(x_loaded, at("x_loaded", a, 16))
                pool.wait_ge(res_ready, at("res_ready", a, 0))
                for j in range(NB):
                    Gp.tensor_tensor(x1[:, j, :], x_in[:, j, :], bo_bc[:], ALU.add).then_inc(x_plus_b, 1)

            def inverse_std2(a, j):
                pool.wait_ge(veps2, at("veps2", a, j + 1))
                Gp.tensor_tensor(rs2[:, j:j + 1], ve2[:, j:j + 1], neg_half[:, 0:1], ALU.pow).then_inc(rstd2, 1)

            def tile(a):
                inverse_std1(a)
                add_bias(a)
                for j in range(NB):
                    inverse_std2(a, j)

            pool.memset(ident[:], 0.0).then_inc(consts_ready, 1)
            pool.memset(neg_half[:], -0.5).then_inc(consts_ready, 1)
            pool.wait_ge(consts_ready, 2)
            pool.affine_select(out=ident[:], in_=ident[:], compare_op=ALU.not_equal, fill=1.0, base=0,
                               pattern=[[-1, P]], channel_multiplier=1).then_inc(consts_ready, 1)
            pool.wait_ge(small_loaded, 80)
            tile(0)
            pool.wait_ge(counted, 1)
            Gp.tensor_reduce(most[:], unequal_sum[:], AX.C, ALU.max).then_inc(low_summed, 1)
            with pool.Fori(1, TILES) as a:
                tile(a)


def kernel(x, ctx_2048, mask_BxS2_fk1, L0_xattn_W_src, L0_xattn_b_src, L0_xattn_W_tgt, L0_xattn_b_tgt,
           L0_xattn_W_out, L0_xattn_b_out, L0_ffn_w1_w, L0_ffn_w1_s, L0_ffn_w2_w, L0_ffn_w2_s, L0_ffn_h1_w,
           L0_ffn_h1_s, L0_ffn_h2_w, L0_ffn_h2_s, L0_ffn_w3_w, L0_ffn_w3_s):
    import concourse.bacc as bacc
    from concourse.bass_utils import run_bass_kernel_spmd

    A = np.asarray

    def by_chunk(w):
        w = A(w).T
        return w.reshape(w.shape[0] // P, P, w.shape[1]).transpose(1, 0, 2)

    def columns(*vs):
        return np.concatenate([A(v).reshape(-1, P).T for v in vs], axis=1)

    Ws, bs = A(L0_xattn_W_src), A(L0_xattn_b_src)
    m = A(mask_BxS2_fk1)
    arrays = {
        "x_t": A(x).reshape(TILES, NB, P, D).transpose(0, 2, 1, 3).reshape(TILES, P, NB * D),
        "ctx_t": A(ctx_2048).reshape(TILES, T, KC, P).transpose(0, 3, 2, 1).reshape(TILES, P, KC * T),
        "mask_row": m.reshape(TILES, T),
        "mask_col": m.reshape(TILES, NB, P).transpose(0, 2, 1),
        "wk": by_chunk(Ws[:D]), "wv": by_chunk(Ws[D:]), "wq": by_chunk(L0_xattn_W_tgt), "wo": by_chunk(L0_xattn_W_out),
        "b_kq": columns(bs[:D], L0_xattn_b_tgt), "b_v": bs[D:].reshape(1, D), "b_o": A(L0_xattn_b_out).reshape(1, D),
        "w1": by_chunk(L0_ffn_w1_w), "w2": by_chunk(L0_ffn_w2_w), "h1": by_chunk(L0_ffn_h1_w),
        "h2": by_chunk(L0_ffn_h2_w), "w3": by_chunk(L0_ffn_w3_w),
        "s_all": columns(L0_ffn_w1_s, L0_ffn_w2_s, L0_ffn_h1_s, L0_ffn_h2_s), "s_3": A(L0_ffn_w3_s).reshape(1, D),
    }
    arrays = {n: np.ascontiguousarray(a) for n, a in arrays.items()}
    nc = bacc.Bacc("TRN2", target_bir_lowering=False, num_devices=1)
    ins = [nc.dram_tensor(n, a.shape, mybir.dt.from_np(a.dtype), kind="ExternalInput").ap() for n, a in arrays.items()]
    out = nc.dram_tensor("out", (B, P, D), F32, kind="ExternalOutput").ap()
    program(nc, *ins, out)
    r = run_bass_kernel_spmd(nc, [arrays], core_ids=[0])
    return r.results[0]["out"]
```

```python
import numpy as np
import concourse.bass as bass
from concourse import mybir
from contextlib import ExitStack
from itertools import islice

F32, F32R, I32 = mybir.dt.float32, mybir.dt.float32r, mybir.dt.int32
ALU, ACT, AX = mybir.AluOpType, mybir.ActivationFunctionType, mybir.AxisListType

P = 128
B, D, DC, HID = 32, 256, 512, 1024
HEADS, DH = 8, 32
NB = 2
T = NB * P
TILES = B // NB
KD, KC, KH = D // P, DC // P, HID // P
ROWS = P // DH
SCALE = 1.0 / float(np.sqrt(DH))
EPS = 1e-5
CH = 1024
CHUNKS = 2 * KD + 2 * KH + KH * D // CH
MASKED = -3.0e38

PER = dict(
    x_loaded=16, ctx_loaded=16, mask_loaded=32,
    xn_ready=2, mask_bias_ready=1, stats1=4, veps1=1, rstd1=1, x_plus_b=2, res_ready=1,
    xt_done=1, k_done=1, q_done=1, v_done=2, xnT_ready=1, kT_ready=2, qT_ready=2, vb_ready=1, v_ready=2,
    scores_done=2, masked=2, max_ready=2, negmax_ready=2, exp_ready=2, recip=2, probs_ready=2,
    pt_done=4, ptA_ready=2, ptV_ready=2, av_done=2, upd_ready=2,
    o_done=2, x1_ready=2, stats2=4, veps2=2, rstd2=2, xn2_ready=2, x2t_done=2, x2hi_ready=2, x2_ready=2,
    gate_done=4, up_done=4, sil_ready=8, g_ready=8, mid_done=8, gelu_ready=16,
    hi_ready=12, h_ready=12, out_done=2, scaled=1, y_ready=2, stored=16,
    block_loaded=16 * 17, block_used=34,
)


def program(nc, x, ctxT, mask_row, mask_col, wsT, wvT, wtT, woT, b_cols, b_v, b_out, w1T, w2T, h1T, h2T,
            w3T, s_cols, s3, out):
    st = ExitStack()
    with st:
        def sb(name, shape, dt=F32):
            return st.enter_context(nc.sbuf_tensor(name, shape, dt))

        W1, W2 = sb("W1", [P, KD, HID], F32R), sb("W2", [P, KD, HID], F32R)
        H1, H2 = sb("H1", [P, KH, HID], F32R), sb("H2", [P, KH, HID], F32R)
        W3 = sb("W3", [P, KH, D], F32R)
        stage = [sb(f"stage{i}", [P, CH]) for i in range(4)]
        WK, WV = sb("WK", [P, KC, D]), sb("WV", [P, KC, D])
        WQ, WO = sb("WQ", [P, KD, D]), sb("WO", [P, 2 * KD, D])
        bcols = sb("bcols", [P, 2 * KD])
        scols = sb("scols", [P, 4 * KH])
        bv_bc, bo_bc, s3_bc = sb("bv_bc", [P, D]), sb("bo_bc", [P, D]), sb("s3_bc", [P, D])
        ident = sb("ident", [P, P])
        neg_half = sb("neg_half", [P, NB])
        unequal, unequal_sum, most = sb("unequal", [P, CHUNKS]), sb("unequal_sum", [P, 1]), sb("most", [1, 1])
        flag = sb("flag", [1, 1], I32)
        x_in, cT = sb("x_in", [P, NB, D]), sb("cT", [P, KC, T])
        mrow, mcol, mbias = sb("mrow", [P, T]), sb("mcol", [P, NB]), sb("mbias", [P, T])
        st1, mv1 = sb("st1", [P, NB, 6]), sb("mv1", [P, NB, 2])
        ve1, rs1 = sb("ve1", [P, NB]), sb("rs1", [P, NB])
        st2, mv2 = sb("st2", [P, NB, 6]), sb("mv2", [P, NB, 2])
        ve2, rs2 = sb("ve2", [P, NB]), sb("rs2", [P, NB])
        xn, xnT = sb("xn", [P, NB, D]), sb("xnT", [P, KD, T])
        kT, qT = sb("kT", [P, KD, T]), sb("qT", [P, KD, T])
        vb, v = sb("vb", [P, NB, D]), sb("v", [P, NB, D])
        pr = [sb(f"pr{j}", [P, ROWS, KD, P]) for j in range(NB)]
        mx, nmx, den, rden = (sb(n, [P, NB, HEADS]) for n in ("mx", "nmx", "den", "rden"))
        pT, upd = sb("pT", [P, KD, ROWS * P]), sb("upd", [P, KD, P])
        x1, res, xn2 = sb("x1", [P, NB, D]), sb("res", [P, NB, D]), sb("xn2", [P, D])
        x2h, x2l = sb("x2h", [P, KD, T], F32R), sb("x2l", [P, KD, T], F32R)
        hAh, hAl = sb("hAh", [P, KH, T], F32R), sb("hAl", [P, KH, T], F32R)
        hBh, hBl = sb("hBh", [P, KH, T], F32R), sb("hBl", [P, KH, T], F32R)
        g, sil_y = sb("g", [P, 2, 2, T]), sb("sil_y", [P, 2 * T + NB * D])
        sil = sil_y[:, 0:2 * T].rearrange("p (h t) -> p h t", h=2)
        y = sil_y[:, 2 * T:].rearrange("p (j n) -> p j n", j=NB)

        F = [st.enter_context(nc.psum_tensor(f"F{i}", [P, 2, T], F32)) for i in range(2)]
        G = [st.enter_context(nc.psum_tensor(f"G{i}", [P, 2 * T], F32)) for i in range(2)]
        S = st.enter_context(nc.psum_tensor("S", [P, ROWS, NB, KD, P], F32))

        landing = [s[:] for s in stage] + [g[:].rearrange("p q h t -> p (q h t)"), sil_y[:]]
        STAGES = len(landing)

        def sem(name):
            return st.enter_context(nc.semaphore(name))

        x_loaded = sem("x_loaded")
        ctx_loaded = sem("ctx_loaded")
        mask_loaded = sem("mask_loaded")
        xn_ready = sem("xn_ready")
        mask_bias_ready = sem("mask_bias_ready")
        stats1 = sem("stats1")
        veps1 = sem("veps1")
        rstd1 = sem("rstd1")
        x_plus_b = sem("x_plus_b")
        res_ready = sem("res_ready")
        xt_done = sem("xt_done")
        k_done = sem("k_done")
        q_done = sem("q_done")
        v_done = sem("v_done")
        xnT_ready = sem("xnT_ready")
        kT_ready = sem("kT_ready")
        qT_ready = sem("qT_ready")
        vb_ready = sem("vb_ready")
        v_ready = sem("v_ready")
        scores_done = sem("scores_done")
        masked = sem("masked")
        max_ready = sem("max_ready")
        negmax_ready = sem("negmax_ready")
        exp_ready = sem("exp_ready")
        recip = sem("recip")
        probs_ready = sem("probs_ready")
        pt_done = sem("pt_done")
        ptA_ready = sem("ptA_ready")
        ptV_ready = sem("ptV_ready")
        av_done = sem("av_done")
        upd_ready = sem("upd_ready")
        o_done = sem("o_done")
        x1_ready = sem("x1_ready")
        stats2 = sem("stats2")
        veps2 = sem("veps2")
        rstd2 = sem("rstd2")
        xn2_ready = sem("xn2_ready")
        x2t_done = sem("x2t_done")
        x2hi_ready = sem("x2hi_ready")
        x2_ready = sem("x2_ready")
        gate_done = sem("gate_done")
        up_done = sem("up_done")
        sil_ready = sem("sil_ready")
        g_ready = sem("g_ready")
        mid_done = sem("mid_done")
        gelu_ready = sem("gelu_ready")
        hi_ready = sem("hi_ready")
        h_ready = sem("h_ready")
        out_done = sem("out_done")
        y_ready = sem("y_ready")
        block_used = sem("block_used")
        scaled = [sem(f"scaled{j}") for j in range(2)]
        stored = [sem(f"stored{j}") for j in range(2)]
        block_loaded = [sem(f"block_loaded{j}") for j in range(2)]
        consts_ready = sem("consts_ready")
        wk_loaded = sem("wk_loaded")
        wq_loaded = sem("wq_loaded")
        wv_loaded = sem("wv_loaded")
        wo_loaded = sem("wo_loaded")
        bias_loaded = sem("bias_loaded")
        small_loaded = sem("small_loaded")
        chunk_cast = sem("chunk_cast")
        chunk_looked = sem("chunk_looked")
        counted = sem("counted")
        low_summed = sem("low_summed")
        flag_ready = sem("flag_ready")
        stats_seen = sem("stats_seen")
        chunk_loaded = [sem(f"chunk_loaded{i}") for i in range(STAGES)]
        def at(name, tile, k):
            value = tile * PER[name] + k
            return max(value, 0) if isinstance(value, int) else value

        chunks = ([(w1T, W1, k) for k in range(KD)] + [(w2T, W2, k) for k in range(KD)]
                  + [(h1T, H1, k) for k in range(KH)] + [(h2T, H2, k) for k in range(KH)]
                  + [(w3T, W3, 4 * k) for k in range(KH * D // CH)])
        assert len(chunks) == CHUNKS
        block = st.enter_context(nc.Block())

        @block.sync
        def _(sp):
            def load_tile(a):
                sp.wait_ge(xn_ready, at("xn_ready", a - 1, 2))
                sp.wait_ge(x_plus_b, at("x_plus_b", a - 1, 2))
                sp.dma_start(x_in[:], x[bass.ds(a, 1)].rearrange("o p n -> (o p) n")).then_inc(x_loaded, 16)
                sp.wait_ge(k_done, at("k_done", a - 1, 1))
                sp.wait_ge(v_done, at("v_done", a - 1, 2))
                sp.dma_start(cT[:], ctxT[bass.ds(a, 1)].rearrange("o p n -> (o p) n")).then_inc(ctx_loaded, 16)
                sp.wait_ge(kT_ready, at("kT_ready", a - 1, 2))
                sp.wait_ge(qT_ready, at("qT_ready", a - 1, 2))
                sp.wait_ge(mask_bias_ready, at("mask_bias_ready", a - 1, 1))
                sp.dma_start(mrow[:], mask_row[bass.ds(a, 1)].broadcast_to([P, T])).then_inc(mask_loaded, 16)
                sp.wait_ge(v_ready, at("v_ready", a - 1, 2))
                sp.dma_start(mcol[:], mask_col[bass.ds(a, 1)].rearrange("o p n -> (o p) n")).then_inc(mask_loaded, 16)

            def raw_block(f, n, src):
                sp.wait_ge(block_used, at("block_used", f, max(n - 1, 0)))
                dst = stage[n % 2][:].rearrange("p (k m) -> p k m", m=src.shape[2])[:, 0:src.shape[1], :]
                sp.dma_start(dst, src).then_inc(block_loaded[n % 2], 16)

            def tile(f, a, general):
                if general:
                    for n in range(2 * KH):
                        src, p = (w1T, w2T)[n // 2 % 2], 2 * (n // 4) + n % 2
                        raw_block(f, n, src[:, :, p * P:(p + 1) * P])
                if a is not None:
                    load_tile(a)
                if general:
                    for m in range(KH):
                        raw_block(f, 16 + m, h1T[:, :, m * P:(m + 1) * P])
                    for m in range(KH):
                        raw_block(f, 24 + m, h2T[:, :, m * P:(m + 1) * P])
                    for n in range(2):
                        raw_block(f, 32 + n, w3T[:, 4 * n:4 * n + 4, :])
                for j in range(NB):
                    sp.wait_ge(y_ready, at("y_ready", f, j + 1))
                    sp.dma_start(out[bass.ds(f * NB + j, 1)].rearrange("o p n -> (o p) n"), y[:, j, :]).then_inc(stored[j], 16)

            def tiles(general):
                tile(0, 2, general)
                with sp.Fori(1, TILES - 2) as i:
                    tile(i, i + 2, general)
                tile(TILES - 2, None, general)
                tile(TILES - 1, None, general)

            sp.dma_start(x_in[:], x[0]).then_inc(x_loaded, 16)
            sp.dma_start(cT[:], ctxT[0]).then_inc(ctx_loaded, 16)
            sp.dma_start(WK[:], wsT).then_inc(wk_loaded, 16)
            sp.dma_start(bcols[:], b_cols).then_inc(bias_loaded, 16)
            sp.dma_start(mrow[:], mask_row[0:1].broadcast_to([P, T])).then_inc(mask_loaded, 16)
            sp.dma_start(mcol[:], mask_col[0]).then_inc(mask_loaded, 16)
            sp.dma_start(WQ[:], wtT).then_inc(wq_loaded, 16)
            sp.dma_start(WV[:], wvT).then_inc(wv_loaded, 16)
            for dst, src in ((scols, s_cols), (bv_bc, b_v.broadcast_to([P, D])),
                             (bo_bc, b_out.broadcast_to([P, D])), (s3_bc, s3.broadcast_to([P, D]))):
                sp.dma_start(dst[:], src).then_inc(small_loaded, 16)
            for n, (src, _, k) in enumerate(chunks):
                if n == 2 * KD:
                    sp.dma_start(WO[:], woT).then_inc(wo_loaded, 16)
                if n == 2 * STAGES:
                    load_tile(1)
                if n >= STAGES:
                    sp.wait_ge(chunk_looked, n - STAGES + 1)
                w = CH // src.shape[2]
                sp.dma_start(landing[n % STAGES].rearrange("p (k m) -> p k m", k=w), src[:, k:k + w, :])\
                    .then_inc(chunk_loaded[n % STAGES], 16)
            sp.wait_ge(flag_ready, 1)
            has_low_bits = sp.value_load(flag[0:1, 0:1], min_val=0, max_val=1)
            with sp.If(has_low_bits):
                tiles(True)
            with sp.Else():
                tiles(False)
            for j in range(NB):
                sp.wait_ge(stored[j], at("stored", TILES, 0))

        @block.tensor
        def _(pe):
            mm = nc.tensor.matmul

            def transposes_x(a):
                pe.wait_ge(xn_ready, at("xn_ready", a, 2))
                pe.wait_ge(x1_ready, at("x1_ready", a - 1, 2))
                for j in range(NB):
                    for c in range(KD):
                        ins = nc.tensor.transpose(G[0][:, c * T + j * P:c * T + (j + 1) * P],
                                                  xn[:, j, c * P:(c + 1) * P], ident[:])
                ins.then_inc(xt_done, 1)

            def project_k(a):
                pe.wait_ge(wk_loaded, 16)
                pe.wait_ge(ctx_loaded, at("ctx_loaded", a, 16))
                pe.wait_ge(x2_ready, at("x2_ready", a - 1, 2))
                for c in range(KD):
                    for k in range(KC):
                        ins = mm(G[1][:, c * T:(c + 1) * T], WK[:, k, c * P:(c + 1) * P], cT[:, k, :],
                                 start=k == 0, stop=k == KC - 1)
                ins.then_inc(k_done, 1)

            def project_q(a):
                pe.wait_ge(xnT_ready, at("xnT_ready", a, 1))
                pe.wait_ge(wq_loaded, 16)
                for c in range(KD):
                    for k in range(KD):
                        ins = mm(G[0][:, c * T:(c + 1) * T], WQ[:, k, c * P:(c + 1) * P], xnT[:, k, :],
                                 start=k == 0, stop=k == KD - 1)
                ins.then_inc(q_done, 1)

            def project_v(a, j):
                pe.wait_ge(wv_loaded, 16)
                pe.wait_ge(kT_ready, at("kT_ready", a, 2))
                for k in range(KC):
                    ins = mm(G[1][:, j * D:(j + 1) * D], cT[:, k, j * P:(j + 1) * P], WV[:, k, :],
                             start=k == 0, stop=k == KC - 1)
                ins.then_inc(v_done, 1)

            def scores(a, j):
                pe.wait_ge(kT_ready, at("kT_ready", a, 2))
                pe.wait_ge(qT_ready, at("qT_ready", a, 2))
                pe.wait_ge(masked, at("masked", a, 0 if j == 0 else 1))
                for c in range(KD):
                    for r in range(ROWS):
                        rows = slice(r * DH, (r + 1) * DH)
                        ins = mm(S[:, r, j, c, :], qT[rows, c, j * P:(j + 1) * P],
                                 kT[rows, c, j * P:(j + 1) * P], start=True, stop=True)
                ins.then_inc(scores_done, 1)

            def transpose_p(a, j):
                pe.wait_ge(probs_ready, at("probs_ready", a, j + 1))
                if j == 0:
                    pe.wait_ge(qT_ready, at("qT_ready", a, 2))
                    pe.wait_ge(vb_ready, at("vb_ready", a, 1))
                else:
                    pe.wait_ge(upd_ready, at("upd_ready", a, 1))
                    pe.wait_ge(ptV_ready, at("ptV_ready", a, 1))
                for c in range(KD):
                    for r in range(ROWS):
                        ins = nc.tensor.transpose(G[c][:, r * P:(r + 1) * P], pr[j][:, r, c, :], ident[:])
                    ins.then_inc(pt_done, 1)

            def attend(a, j):
                pe.wait_ge(v_ready, at("v_ready", a, 2))
                pe.wait_ge(ptA_ready, at("ptA_ready", a, j + 1))
                for c in range(KD):
                    if c == 1:
                        pe.wait_ge(ptV_ready, at("ptV_ready", a, j + 1))
                    for r in range(ROWS):
                        h = c * ROWS + r
                        ins = mm(G[0][r * DH:(r + 1) * DH, c * P:(c + 1) * P], v[:, j, h * DH:(h + 1) * DH],
                                 pT[:, c, r * P:(r + 1) * P], start=True, stop=True)
                ins.then_inc(av_done, 1)

            def out_proj(a, j):
                bank = G[1] if j == 0 else G[0]
                if j == 0:
                    pe.wait_ge(ptV_ready, at("ptV_ready", a, 2))
                pe.wait_ge(upd_ready, at("upd_ready", a, j + 1))
                pe.wait_ge(wo_loaded, 16)
                for k in range(2 * KD):
                    lhsT = xnT[:, k, j * P:(j + 1) * P] if k < KD else upd[:, k - KD, :]
                    ins = mm(bank[:, 0:D], lhsT, WO[:, k, :], start=k == 0, stop=k == 2 * KD - 1)
                ins.then_inc(o_done, 1)

            def transpose_x2(a, j):
                pe.wait_ge(xn2_ready, at("xn2_ready", a, j + 1))
                if j == 0:
                    pe.wait_ge(x1_ready, at("x1_ready", a, 1))
                else:
                    pe.wait_ge(x2_ready, at("x2_ready", a, 1))
                for c in range(KD):
                    ins = nc.tensor.transpose(G[1][:, c * P:(c + 1) * P], xn2[:, c * P:(c + 1) * P], ident[:])
                ins.then_inc(x2t_done, 1)

            def ffn_group(bank, W, cols, parts, general, f, n, ready=None):
                kk = W.shape[1]
                if general:
                    pe.wait_ge(block_loaded[n % 2], at("block_loaded", f, 16 * (n // 2 + 1)))
                    raw = stage[n % 2][:].rearrange("p (k m) -> p k m", m=P)
                for k in range(kk):
                    if ready is not None:
                        ready(k)
                    for q, part in enumerate(parts):
                        first, last = k == 0 and q == 0, k == kk - 1 and q == 1
                        if general:
                            ins = mm(bank, raw[:, k, :], part[:, k, :].bitcast(F32), start=first, stop=last)
                        else:
                            ins = mm(bank, W[:, k, cols], part[:, k, :], start=first, stop=last)
                if general:
                    ins.then_inc(block_used, 1)
                    ins = pe.nop()
                return ins

            def gate_up(f, q, general):
                pe.wait_ge(x2_ready, at("x2_ready", f, 2))
                if q == 0:
                    pe.wait_ge(scaled[0], at("scaled", f - 1, 1))
                else:
                    pe.wait_ge(sil_ready, at("sil_ready", f, 2 * q))
                for h in range(2):
                    cols = slice((2 * q + h) * P, (2 * q + h + 1) * P)
                    ins = ffn_group(F[0][:, h, :], W1, cols, (x2h, x2l), general, f, 4 * q + h)
                ins.then_inc(gate_done, 1)
                if q == 0:
                    pe.wait_ge(scaled[1], at("scaled", f - 1, 1))
                else:
                    pe.wait_ge(g_ready, at("g_ready", f, 2 * q))
                for h in range(2):
                    cols = slice((2 * q + h) * P, (2 * q + h + 1) * P)
                    ins = ffn_group(F[1][:, h, :], W2, cols, (x2h, x2l), general, f, 4 * q + 2 + h)
                ins.then_inc(up_done, 1)

            def middle(f, q, half, general):
                W, parts = (H1, (hAh, hAl)) if q < 8 else (H2, (hBh, hBl))
                if half == 0 and q == 4:
                    pe.wait_ge(sil_ready, at("sil_ready", f, KH))
                elif half == 0 and q == 5:
                    pe.wait_ge(g_ready, at("g_ready", f, KH))
                elif half == 0:
                    pe.wait_ge(gelu_ready, at("gelu_ready", f, 2 * (q - 5)))
                m = 2 * (q % 4) + half

                def ready(k):
                    if m == 0 and k % 2 == 0:
                        pe.wait_ge(h_ready, at("h_ready", f, q - 4 + k // 2 + 1))

                ins = ffn_group(F[q % 2][:, half, :], W, slice(m * P, (m + 1) * P), parts, general, f,
                                2 * KH + (q // 4 - 1) * KH + m, ready)
                if half:
                    ins.then_inc(mid_done, 1)

            def ffn_out(f, general):
                if general:
                    for n in range(2):
                        pe.wait_ge(block_loaded[n], at("block_loaded", f, 16 * (2 * KH + 1)))
                for j, ks in ((0, range(6)), (1, range(6)), (0, (6, 7)), (1, (6, 7))):
                    if ks[0] == 0:
                        pe.wait_ge(gelu_ready, at("gelu_ready", f, 14 + 2 * j))
                    for k in ks:
                        if j == 0 and k % 2 == 0:
                            pe.wait_ge(h_ready, at("h_ready", f, 8 + k // 2 + 1))
                        for q, h in enumerate((hAh, hAl)):
                            first, last = k == 0 and q == 0, k == KH - 1 and q == 1
                            lhsT = h[:, k, j * P:(j + 1) * P]
                            if general:
                                raw = stage[k // 4][:, k % 4 * D:(k % 4 + 1) * D]
                                ins = mm(F[j][:, 0, :], lhsT.bitcast(F32), raw, start=first, stop=last)
                            else:
                                ins = mm(F[j][:, 0, :], lhsT, W3[:, k, :], start=first, stop=last)
                    if ks[-1] == KH - 1:
                        ins.then_inc(out_done, 1)
                if general:
                    pe.wait_ge(out_done, at("out_done", f, 2))
                    pe.sem_inc(block_used, 2)

            def tile(f, a, general):
                attn, ffn = a is not None, f is not None
                if attn:
                    transposes_x(a)
                for q in range(4):
                    if ffn:
                        gate_up(f, q, general)
                    if attn and q == 0:
                        project_k(a)
                        project_q(a)
                    if attn and q == 1:
                        scores(a, 0)
                    if attn and q == 2:
                        scores(a, 1)
                    if attn and q == 3:
                        project_v(a, 0)
                        project_v(a, 1)
                for q in range(4, 12):
                    for half in range(2):
                        if attn and (q, half) == (6, 0):
                            transpose_p(a, 0)
                        if attn and (q, half) == (7, 0):
                            attend(a, 0)
                        if attn and (q, half) == (7, 1):
                            transpose_p(a, 1)
                        if attn and (q, half) == (8, 0):
                            attend(a, 1)
                            out_proj(a, 0)
                        if attn and (q, half) == (9, 1):
                            out_proj(a, 1)
                        if attn and (q, half) == (10, 0):
                            transpose_x2(a, 0)
                        if attn and (q, half) == (11, 1):
                            transpose_x2(a, 1)
                        if ffn:
                            middle(f, q, half, general)
                if ffn:
                    ffn_out(f, general)

            def tiles(general):
                tile(0, 1, general)
                with pe.Fori(1, TILES - 1) as i:
                    tile(i, i + 1, general)
                tile(TILES - 1, None, general)

            pe.wait_ge(consts_ready, 3)
            tile(None, 0, False)
            pe.wait_ge(flag_ready, 1)
            has_low_bits = pe.value_load(flag[0:1, 0:1], min_val=0, max_val=1)
            with pe.If(has_low_bits):
                tiles(True)
            with pe.Else():
                tiles(False)

        @block.scalar
        def _(act):
            fn = nc.scalar.activation

            def silu(f, q):
                act.wait_ge(gate_done, at("gate_done", f, q + 1))
                for p in (2 * q, 2 * q + 1):
                    act.wait_ge(g_ready, at("g_ready", f, max(p - 1, 0)))
                    fn(sil[:, p % 2, :], F[0][:, p % 2, :], ACT.Silu, scale=scols[:, p:p + 1]).then_inc(sil_ready, 1)

            def gelu(f, q):
                act.wait_ge(mid_done, at("mid_done", f, q - 3))
                act.wait_ge(h_ready, at("h_ready", f, q - 1))
                for m in (0, 1):
                    col = KH + 2 * q + m
                    fn(g[:, q % 2, m, :], F[q % 2][:, m, :], ACT.Gelu, scale=scols[:, col:col + 1]).then_inc(gelu_ready, 1)

            def copy_xnT(a):
                act.wait_ge(xt_done, at("xt_done", a, 1))
                act.wait_ge(o_done, at("o_done", a - 1, 2))
                fn(xnT[:].rearrange("p c t -> p (c t)"), G[0][:], ACT.Copy).then_inc(xnT_ready, 1)

            def exps(a, j):
                act.wait_ge(negmax_ready, at("negmax_ready", a, j + 1))
                for r in range(ROWS):
                    for c in range(KD):
                        h = r * KD + c
                        ins = fn(pr[j][:, r, c, :], pr[j][:, r, c, :], ACT.Exp, bias=nmx[:, j, h:h + 1],
                                 scale=SCALE, accum_out=den[:, j, h:h + 1])
                ins.then_inc(exp_ready, 1)

            def scale_v(a):
                act.wait_ge(vb_ready, at("vb_ready", a, 1))
                act.wait_ge(mask_loaded, at("mask_loaded", a, 32))
                act.wait_ge(av_done, at("av_done", a - 1, 2))
                for j in range(NB):
                    fn(v[:, j, :], vb[:, j, :], ACT.Copy, scale=mcol[:, j:j + 1]).then_inc(v_ready, 1)

            def copy_pT(a, j):
                act.wait_ge(pt_done, at("pt_done", a, 2 * j + 1))
                act.wait_ge(av_done, at("av_done", a, j))
                fn(pT[:, 0, :], G[0][:], ACT.Copy).then_inc(ptA_ready, 1)

            def copy_upd(a, j):
                act.wait_ge(av_done, at("av_done", a, j + 1))
                act.wait_ge(o_done, at("o_done", a, j))
                fn(upd[:].rearrange("p c t -> p (c t)"), G[0][:, 0:KD * P], ACT.Copy).then_inc(upd_ready, 1)

            def x2_hi(a, j):
                act.wait_ge(x2t_done, at("x2t_done", a, j + 1))
                act.wait_ge(up_done, at("up_done", a - 1, 4))
                fn(x2h[:, :, j * P:(j + 1) * P], G[1][:, 0:KD * P].rearrange("p (c t) -> p c t", c=KD), ACT.Copy).then_inc(x2hi_ready, 1)

            def tile(f, a):
                attn, ffn = a is not None, f is not None
                left = iter(range(0 if ffn else CHUNKS))

                def casts(count):
                    for n in islice(left, count):
                        cast(n)

                if attn:
                    copy_xnT(a)
                    casts(4)
                if ffn:
                    for q in range(4):
                        silu(f, q)
                if attn:
                    exps(a, 0)
                    casts(1)
                    exps(a, 1)
                    casts(2)
                for q in range(4, 12):
                    if attn and q == 6:
                        scale_v(a)
                        copy_pT(a, 0)
                        casts(2)
                    if attn and q == 7:
                        copy_upd(a, 0)
                        casts(1)
                        copy_pT(a, 1)
                        casts(2)
                    if attn and q == 8:
                        copy_upd(a, 1)
                        casts(3)
                    if attn and q == 10:
                        x2_hi(a, 0)
                        casts(1)
                    if attn and q == 11:
                        x2_hi(a, 1)
                        casts(CHUNKS)
                    if ffn:
                        gelu(f, q)

            def cast(n):
                _, W, k = chunks[n]
                w = CH // W.shape[2]
                act.wait_ge(chunk_loaded[n % STAGES], 16 * (n // STAGES + 1))
                fn(W[:, k:k + w, :], landing[n % STAGES].rearrange("p (k m) -> p k m", k=w), ACT.Copy)\
                    .then_inc(chunk_cast, 1)

            act.wait_ge(small_loaded, 64)
            tile(None, 0)
            tile(0, 1)
            with act.Fori(1, TILES - 1) as i:
                tile(i, i + 1)
            tile(TILES - 1, None)

        @block.vector
        def _(dve):
            V = nc.vector

            def keep_residual(f):
                dve.wait_ge(x1_ready, at("x1_ready", f, 2))
                dve.wait_ge(y_ready, at("y_ready", f - 1, 2))
                V.tensor_copy(res[:], x1[:]).then_inc(res_ready, 1)

            def ln1_stats(a):
                dve.wait_ge(x_loaded, at("x_loaded", a, 16))
                for j in range(NB):
                    V.bn_stats(st1[:, j, :], x_in[:, j, :]).then_inc(stats1, 1)
                dve.wait_ge(stats1, at("stats1", a, 2))
                dve.sem_inc(stats_seen, 1)
                for j in range(NB):
                    V.bn_aggr(mv1[:, j, :], st1[:, j, :]).then_inc(stats1, 1)
                dve.wait_ge(stats1, at("stats1", a, 4))
                V.tensor_scalar_add(ve1[:], mv1[:, :, 1], EPS).then_inc(veps1, 1)

            def mask_bias(a):
                dve.wait_ge(mask_loaded, at("mask_loaded", a, 32))
                V.tensor_scalar(mbias[:], mrow[:], 0.0, MASKED, ALU.is_equal, ALU.mult).then_inc(mask_bias_ready, 1)

            def ln1_apply(a):
                dve.wait_ge(rstd1, at("rstd1", a, 1))
                dve.wait_ge(xt_done, at("xt_done", a - 1, 1))
                for j in range(NB):
                    V.tensor_scalar(xn[:, j, :], x_in[:, j, :], mv1[:, j, 0:1], rs1[:, j:j + 1],
                                        ALU.subtract, ALU.mult).then_inc(xn_ready, 1)

            def bias_mask_k(a):
                dve.wait_ge(k_done, at("k_done", a, 1))
                dve.wait_ge(mask_loaded, at("mask_loaded", a, 32))
                dve.wait_ge(scores_done, at("scores_done", a - 1, 2))
                for c in range(KD):
                    V.scalar_tensor_tensor(kT[:, c, :], G[1][:, c * T:(c + 1) * T], bcols[:, c:c + 1],
                                           mrow[:], ALU.add, ALU.mult).then_inc(kT_ready, 1)

            def bias_mask_q(a):
                dve.wait_ge(q_done, at("q_done", a, 1))
                dve.wait_ge(mask_loaded, at("mask_loaded", a, 32))
                dve.wait_ge(scores_done, at("scores_done", a - 1, 2))
                for c in range(KD):
                    V.scalar_tensor_tensor(qT[:, c, :], G[0][:, c * T:(c + 1) * T], bcols[:, KD + c:KD + c + 1],
                                           mrow[:], ALU.add, ALU.mult).then_inc(qT_ready, 1)

            def bias_v(a):
                dve.wait_ge(v_done, at("v_done", a, 2))
                dve.wait_ge(v_ready, at("v_ready", a - 1, 2))
                dve.wait_ge(small_loaded, 64)
                V.tensor_tensor(vb[:], G[1][:].rearrange("p (j n) -> p j n", j=NB),
                                    bv_bc[:].unsqueeze(1).broadcast_to([P, NB, D]), ALU.add).then_inc(vb_ready, 1)

            def mask_scores(a, j):
                dve.wait_ge(scores_done, at("scores_done", a, j + 1))
                dve.wait_ge(pt_done, at("pt_done", a - 1, 2 * j + 2))
                dve.wait_ge(mask_bias_ready, at("mask_bias_ready", a, 1))
                bias = mbias[:, j * P:(j + 1) * P].unsqueeze(1).unsqueeze(1).broadcast_to([P, ROWS, KD, P])
                V.tensor_tensor(pr[j][:], S[:, :, j, :, :], bias, ALU.add).then_inc(masked, 1)

            def row_max(a, j):
                dve.wait_ge(masked, at("masked", a, j + 1))
                V.tensor_reduce(mx[:, j, :], pr[j][:].rearrange("p r c s -> p (r c) s"), AX.X, ALU.max).then_inc(max_ready, 1)
                dve.wait_ge(max_ready, at("max_ready", a, j + 1))
                dve.wait_ge(exp_ready, at("exp_ready", a - 1, j + 1))
                V.tensor_scalar_mul(nmx[:, j, :], mx[:, j, :], -SCALE).then_inc(negmax_ready, 1)

            def normalise(a, j):
                dve.wait_ge(exp_ready, at("exp_ready", a, j + 1))
                V.reciprocal(rden[:, j, :], den[:, j, :]).then_inc(recip, 1)
                dve.wait_ge(recip, at("recip", a, j + 1))
                p8 = pr[j][:].rearrange("p r c s -> p (r c) s")
                V.tensor_tensor(p8, p8, rden[:, j, :].unsqueeze(2).broadcast_to([P, HEADS, P]), ALU.mult).then_inc(probs_ready, 1)

            def copy_pT(a, j):
                dve.wait_ge(pt_done, at("pt_done", a, 2 * j + 2))
                dve.wait_ge(av_done, at("av_done", a, j))
                V.tensor_copy(pT[:, 1, :], G[1][:]).then_inc(ptV_ready, 1)

            def residual_ln2_stats(a, j):
                bank = G[1] if j == 0 else G[0]
                dve.wait_ge(o_done, at("o_done", a, j + 1))
                dve.wait_ge(x_plus_b, at("x_plus_b", a, j + 1))
                V.tensor_tensor(x1[:, j, :], bank[:, 0:D], x1[:, j, :], ALU.add).then_inc(x1_ready, 1)
                dve.wait_ge(x1_ready, at("x1_ready", a, j + 1))
                V.bn_stats(st2[:, j, :], x1[:, j, :]).then_inc(stats2, 1)
                dve.wait_ge(stats2, at("stats2", a, 2 * j + 1))
                dve.sem_inc(stats_seen, 1)
                V.bn_aggr(mv2[:, j, :], st2[:, j, :]).then_inc(stats2, 1)
                dve.wait_ge(stats2, at("stats2", a, 2 * j + 2))
                V.tensor_scalar_add(ve2[:, j:j + 1], mv2[:, j, 1:2], EPS).then_inc(veps2, 1)

            def ln2_apply(a, j):
                dve.wait_ge(rstd2, at("rstd2", a, j + 1))
                dve.wait_ge(x2t_done, at("x2t_done", a, j))
                V.tensor_scalar(xn2[:], x1[:, j, :], mv2[:, j, 0:1], rs2[:, j:j + 1],
                                    ALU.subtract, ALU.mult).then_inc(xn2_ready, 1)

            def x2_lo(a, j):
                dve.wait_ge(x2hi_ready, at("x2hi_ready", a, j + 1))
                dve.wait_ge(up_done, at("up_done", a - 1, 4))
                part = slice(j * P, (j + 1) * P)
                V.tensor_tensor(x2l[:, :, part], G[1][:, 0:KD * P].rearrange("p (c t) -> p c t", c=KD),
                                    x2h[:, :, part].bitcast(F32), ALU.subtract).then_inc(x2_ready, 1)

            def gate_times_up(f, q):
                dve.wait_ge(up_done, at("up_done", f, q + 1))
                dve.wait_ge(h_ready, at("h_ready", f, max(q - 1, 0)))
                for p in (2 * q, 2 * q + 1):
                    dve.wait_ge(sil_ready, at("sil_ready", f, p + 1))
                    V.scalar_tensor_tensor(g[:, q % 2, p % 2, :], F[1][:, p % 2, :], scols[:, KH + p:KH + p + 1],
                                               sil[:, p % 2, :], ALU.mult, ALU.mult).then_inc(g_ready, 1)

            def split(f, q):
                hi, lo = ((hAh, hAl), (hBh, hBl), (hAh, hAl))[q // 4]
                pair = slice(2 * (q % 4), 2 * (q % 4) + 2)
                if q < 4:
                    dve.wait_ge(g_ready, at("g_ready", f, 2 * q + 2))
                    dve.wait_ge(out_done, at("out_done", f - 1, 2))
                elif q < 8:
                    dve.wait_ge(gelu_ready, at("gelu_ready", f, 2 * (q - 4) + 2))
                    dve.wait_ge(mid_done, at("mid_done", f - 1, 8))
                else:
                    dve.wait_ge(gelu_ready, at("gelu_ready", f, 2 * (q - 4) + 2))
                    dve.wait_ge(mid_done, at("mid_done", f, 4))
                V.tensor_copy(hi[:, pair, :], g[:, q % 2, :, :]).then_inc(hi_ready, 1)
                dve.wait_ge(hi_ready, at("hi_ready", f, q + 1))
                V.tensor_tensor(lo[:, pair, :], g[:, q % 2, :, :], hi[:, pair, :].bitcast(F32), ALU.subtract).then_inc(h_ready, 1)

            def scale_out(f, j):
                dve.wait_ge(out_done, at("out_done", f, j + 1))
                dve.wait_ge(stored[j], at("stored", f - 1, 16))
                V.tensor_tensor(y[:, j, :], F[j][:, 0, :], s3_bc[:], ALU.mult).then_inc(scaled[j], 1)

            def add_residual(f, j):
                dve.wait_ge(scaled[j], at("scaled", f, 1))
                V.tensor_tensor(y[:, j, :], y[:, j, :], res[:, j, :], ALU.add).then_inc(y_ready, 1)

            def tile(f, a, following):
                attn, ffn = a is not None, f is not None
                left = iter(range(0 if ffn else CHUNKS))

                def looks(count):
                    for n in islice(left, count):
                        look(n)

                if ffn:
                    keep_residual(f)
                if attn:
                    mask_bias(a)
                for q in range(4):
                    if ffn:
                        gate_times_up(f, q)
                    if attn and q == 2:
                        row_max(a, 0)
                        looks(2)
                    if ffn:
                        split(f, q)
                    if attn and q == 0:
                        bias_mask_k(a)
                        bias_mask_q(a)
                        looks(2)
                    if attn and q in (1, 2):
                        mask_scores(a, q - 1)
                if attn:
                    row_max(a, 1)
                    normalise(a, 0)
                    bias_v(a)
                    looks(2)
                for q in range(4, 12):
                    if attn and q == 6:
                        copy_pT(a, 0)
                        normalise(a, 1)
                        looks(2)
                    if attn and q == 7:
                        copy_pT(a, 1)
                        looks(4)
                    if attn and q == 8:
                        residual_ln2_stats(a, 0)
                        ln2_apply(a, 0)
                    if attn and q == 9:
                        residual_ln2_stats(a, 1)
                        looks(1)
                    if attn and q == 10:
                        x2_lo(a, 0)
                        ln2_apply(a, 1)
                        looks(2)
                    if attn and q == 11:
                        x2_lo(a, 1)
                        looks(3)
                    if ffn:
                        split(f, q)
                    if following is not None and q == (10 if ffn else 9):
                        ln1_stats(following)
                    if following is not None and q == (11 if ffn else 10):
                        ln1_apply(following)
                if attn:
                    looks(CHUNKS)
                if ffn:
                    scale_out(f, 0)
                    scale_out(f, 1)
                    add_residual(f, 0)
                    add_residual(f, 1)

            def look(n):
                _, W, k = chunks[n]
                w = CH // W.shape[2]
                raw = landing[n % STAGES].rearrange("p (k m) -> p k m", k=w)
                dve.wait_ge(chunk_cast, n + 1)
                V.scalar_tensor_tensor(raw, raw, 1.0, W[:, k:k + w, :].bitcast(F32), ALU.mult, ALU.not_equal,
                                       accum_out=unequal[:, n:n + 1]).then_inc(chunk_looked, 1)

            ln1_stats(0)
            ln1_apply(0)
            dve.wait_ge(bias_loaded, 16)
            tile(None, 0, 1)
            dve.wait_ge(chunk_looked, CHUNKS)
            V.tensor_reduce(unequal_sum[:], unequal[:], AX.X, ALU.max).then_inc(counted, 1)
            dve.wait_ge(low_summed, 1)
            V.tensor_scalar_min(flag[:], most[:], 1.0).then_inc(flag_ready, 1)
            tile(0, 1, 2)
            with dve.Fori(1, TILES - 2) as i:
                tile(i, i + 1, i + 2)
            tile(TILES - 2, TILES - 1, None)
            tile(TILES - 1, None, None)

        @block.gpsimd
        def _(pool):
            Gp = nc.gpsimd

            def inverse_std1(a):
                pool.wait_ge(veps1, at("veps1", a, 1))
                Gp.tensor_tensor(rs1[:], ve1[:], neg_half[:], ALU.pow).then_inc(rstd1, 1)

            def add_bias(a):
                pool.wait_ge(x_loaded, at("x_loaded", a, 16))
                pool.wait_ge(res_ready, at("res_ready", a, 0))
                for j in range(NB):
                    Gp.tensor_tensor(x1[:, j, :], x_in[:, j, :], bo_bc[:], ALU.add).then_inc(x_plus_b, 1)

            def inverse_std2(a, j):
                pool.wait_ge(veps2, at("veps2", a, j + 1))
                Gp.tensor_tensor(rs2[:, j:j + 1], ve2[:, j:j + 1], neg_half[:, 0:1], ALU.pow).then_inc(rstd2, 1)

            def tile(a, following):
                add_bias(a)
                for j in range(NB):
                    inverse_std2(a, j)
                if following is not None:
                    inverse_std1(following)

            pool.memset(ident[:], 0.0).then_inc(consts_ready, 1)
            pool.memset(neg_half[:], -0.5).then_inc(consts_ready, 1)
            pool.wait_ge(consts_ready, 2)
            pool.affine_select(out=ident[:], in_=ident[:], compare_op=ALU.not_equal, fill=1.0, base=0,
                               pattern=[[-1, P]], channel_multiplier=1).then_inc(consts_ready, 1)
            inverse_std1(0)
            pool.wait_ge(small_loaded, 64)
            tile(0, 1)
            pool.wait_ge(counted, 1)
            Gp.tensor_reduce(most[:], unequal_sum[:], AX.C, ALU.max).then_inc(low_summed, 1)
            with pool.Fori(1, TILES - 1) as a:
                tile(a, a + 1)
            tile(TILES - 1, None)


def kernel(x, ctx_2048, mask_BxS2_fk1, L0_xattn_W_src, L0_xattn_b_src, L0_xattn_W_tgt, L0_xattn_b_tgt,
           L0_xattn_W_out, L0_xattn_b_out, L0_ffn_w1_w, L0_ffn_w1_s, L0_ffn_w2_w, L0_ffn_w2_s, L0_ffn_h1_w,
           L0_ffn_h1_s, L0_ffn_h2_w, L0_ffn_h2_s, L0_ffn_w3_w, L0_ffn_w3_s):
    import concourse.bacc as bacc
    from concourse.bass_utils import run_bass_kernel_spmd

    A = np.asarray

    def by_chunk(w):
        w = A(w).T
        return w.reshape(w.shape[0] // P, P, w.shape[1]).transpose(1, 0, 2)

    def columns(*vs):
        return np.concatenate([A(v).reshape(-1, P).T for v in vs], axis=1)

    Ws, bs = A(L0_xattn_W_src), A(L0_xattn_b_src)
    m = A(mask_BxS2_fk1)
    arrays = {
        "x_t": A(x).reshape(TILES, NB, P, D).transpose(0, 2, 1, 3).reshape(TILES, P, NB * D),
        "ctx_t": A(ctx_2048).reshape(TILES, T, KC, P).transpose(0, 3, 2, 1).reshape(TILES, P, KC * T),
        "mask_row": m.reshape(TILES, T),
        "mask_col": m.reshape(TILES, NB, P).transpose(0, 2, 1),
        "wk": by_chunk(Ws[:D]), "wv": by_chunk(Ws[D:]), "wq": by_chunk(L0_xattn_W_tgt), "wo": by_chunk(L0_xattn_W_out),
        "b_kq": columns(bs[:D], L0_xattn_b_tgt), "b_v": bs[D:].reshape(1, D), "b_o": A(L0_xattn_b_out).reshape(1, D),
        "w1": by_chunk(L0_ffn_w1_w), "w2": by_chunk(L0_ffn_w2_w), "h1": by_chunk(L0_ffn_h1_w),
        "h2": by_chunk(L0_ffn_h2_w), "w3": by_chunk(L0_ffn_w3_w),
        "s_all": columns(L0_ffn_w1_s, L0_ffn_w2_s, L0_ffn_h1_s, L0_ffn_h2_s), "s_3": A(L0_ffn_w3_s).reshape(1, D),
    }
    arrays = {n: np.ascontiguousarray(a) for n, a in arrays.items()}
    nc = bacc.Bacc("TRN2", target_bir_lowering=False, num_devices=1)
    ins = [nc.dram_tensor(n, a.shape, mybir.dt.from_np(a.dtype), kind="ExternalInput").ap() for n, a in arrays.items()]
    out = nc.dram_tensor("out", (B, P, D), F32, kind="ExternalOutput").ap()
    program(nc, *ins, out)
    r = run_bass_kernel_spmd(nc, [arrays], core_ids=[0])
    return r.results[0]["out"]
```

```python
import numpy as np
import concourse.bass as bass
from concourse import mybir
from contextlib import ExitStack
from itertools import islice

F32, F32R, I32 = mybir.dt.float32, mybir.dt.float32r, mybir.dt.int32
ALU, ACT, AX = mybir.AluOpType, mybir.ActivationFunctionType, mybir.AxisListType

P = 128
B, D, DC, HID = 32, 256, 512, 1024
HEADS, DH = 8, 32
NB = 2
T = NB * P
TILES = B // NB
KD, KC, KH = D // P, DC // P, HID // P
ROWS = P // DH
SCALE = 1.0 / float(np.sqrt(DH))
EPS = 1e-5
CH = 1024
CHUNKS = 2 * KD + 2 * KH + KH * D // CH
LATE = 6
EARLY = CHUNKS - LATE
MASKED = -3.0e38

PER = dict(
    x_loaded=16, ctx_loaded=16, mask_loaded=32,
    xn_ready=2, mask_bias_ready=1, stats1=4, veps1=1, rstd1=1, x_plus_b=2, res_ready=1,
    xt_done=1, k_done=1, q_done=1, v_done=2, xnT_ready=1, kT_ready=2, qT_ready=2, vb_ready=1, v_ready=2,
    scores_done=2, masked=2, max_ready=2, negmax_ready=2, exp_ready=2, recip=2, probs_ready=2,
    pt_done=4, ptA_ready=2, ptV_ready=2, av_done=2, upd_ready=2,
    o_done=2, x1_ready=2, stats2=4, veps2=2, rstd2=2, xn2_ready=2, x2t_done=2, x2hi_ready=2, x2_ready=2,
    gate_done=4, up_done=4, sil_ready=8, g_ready=8, mid_done=8, gelu_ready=16,
    hi_ready=12, h_ready=12, out_done=2, scaled=1, y_ready=2, stored=16,
    block_loaded=16 * 17, block_used=34,
)


def program(nc, x, ctxT, mask_row, mask_col, wsT, wvT, wtT, woT, b_cols, b_v, b_out, w1T, w2T, h1T, h2T,
            w3T, s_cols, s3, out):
    st = ExitStack()
    with st:
        def sb(name, shape, dt=F32):
            return st.enter_context(nc.sbuf_tensor(name, shape, dt))

        W1, W2 = sb("W1", [P, KD, HID], F32R), sb("W2", [P, KD, HID], F32R)
        H1, H2 = sb("H1", [P, KH, HID], F32R), sb("H2", [P, KH, HID], F32R)
        W3 = sb("W3", [P, KH, D], F32R)
        stage = [sb(f"stage{i}", [P, CH]) for i in range(4)]
        WK, WV = sb("WK", [P, KC, D]), sb("WV", [P, KC, D])
        WQ, WO = sb("WQ", [P, KD, D]), sb("WO", [P, 2 * KD, D])
        bcols = sb("bcols", [P, 2 * KD])
        scols = sb("scols", [P, 4 * KH])
        bv_bc, bo_bc, s3_bc = sb("bv_bc", [P, D]), sb("bo_bc", [P, D]), sb("s3_bc", [P, D])
        ident = sb("ident", [P, P])
        neg_half = sb("neg_half", [P, NB])
        unequal, unequal_sum, most = sb("unequal", [P, CHUNKS]), sb("unequal_sum", [P, 2]), sb("most", [1, 2])
        flag = sb("flag", [1, 2], I32)
        x_in, cT = sb("x_in", [P, NB, D]), sb("cT", [P, KC, T])
        mrow, mcol, mbias = sb("mrow", [P, T]), sb("mcol", [P, NB]), sb("mbias", [P, T])
        st1, mv1 = sb("st1", [P, NB, 6]), sb("mv1", [P, NB, 2])
        ve1, rs1 = sb("ve1", [P, NB]), sb("rs1", [P, NB])
        st2, mv2 = sb("st2", [P, NB, 6]), sb("mv2", [P, NB, 2])
        ve2, rs2 = sb("ve2", [P, NB]), sb("rs2", [P, NB])
        xn, xnT = sb("xn", [P, NB, D]), sb("xnT", [P, KD, T])
        kT, qT = sb("kT", [P, KD, T]), sb("qT", [P, KD, T])
        vb, v = sb("vb", [P, NB, D]), sb("v", [P, NB, D])
        pr = [sb(f"pr{j}", [P, ROWS, KD, P]) for j in range(NB)]
        mx, nmx, den, rden = (sb(n, [P, NB, HEADS]) for n in ("mx", "nmx", "den", "rden"))
        pT, upd = sb("pT", [P, KD, ROWS * P]), sb("upd", [P, KD, P])
        x1, res, xn2 = sb("x1", [P, NB, D]), sb("res", [P, NB, D]), sb("xn2", [P, D])
        x2h, x2l = sb("x2h", [P, KD, T], F32R), sb("x2l", [P, KD, T], F32R)
        hAh, hAl = sb("hAh", [P, KH, T], F32R), sb("hAl", [P, KH, T], F32R)
        hBh, hBl = sb("hBh", [P, KH, T], F32R), sb("hBl", [P, KH, T], F32R)
        g, sil_y = sb("g", [P, 2, 2, T]), sb("sil_y", [P, 2 * T + NB * D])
        sil = sil_y[:, 0:2 * T].rearrange("p (h t) -> p h t", h=2)
        y = sil_y[:, 2 * T:].rearrange("p (j n) -> p j n", j=NB)

        F = [st.enter_context(nc.psum_tensor(f"F{i}", [P, 2, T], F32)) for i in range(2)]
        G = [st.enter_context(nc.psum_tensor(f"G{i}", [P, 2 * T], F32)) for i in range(2)]
        S = st.enter_context(nc.psum_tensor("S", [P, ROWS, NB, KD, P], F32))

        landing = [s[:] for s in stage] + [g[:].rearrange("p q h t -> p (q h t)"), sil_y[:]]
        land = [n % len(landing) for n in range(EARLY)] + [4, 5, 2, 3, 2, 3]
        assert len(land) == CHUNKS

        def landed(n):
            return 16 * land[:n + 1].count(land[n])

        def sem(name):
            return st.enter_context(nc.semaphore(name))

        x_loaded = sem("x_loaded")
        ctx_loaded = sem("ctx_loaded")
        mask_loaded = sem("mask_loaded")
        xn_ready = sem("xn_ready")
        mask_bias_ready = sem("mask_bias_ready")
        stats1 = sem("stats1")
        veps1 = sem("veps1")
        rstd1 = sem("rstd1")
        x_plus_b = sem("x_plus_b")
        res_ready = sem("res_ready")
        xt_done = sem("xt_done")
        k_done = sem("k_done")
        q_done = sem("q_done")
        v_done = sem("v_done")
        xnT_ready = sem("xnT_ready")
        kT_ready = sem("kT_ready")
        qT_ready = sem("qT_ready")
        vb_ready = sem("vb_ready")
        v_ready = sem("v_ready")
        scores_done = sem("scores_done")
        masked = sem("masked")
        max_ready = sem("max_ready")
        negmax_ready = sem("negmax_ready")
        exp_ready = sem("exp_ready")
        recip = sem("recip")
        probs_ready = sem("probs_ready")
        pt_done = sem("pt_done")
        ptA_ready = sem("ptA_ready")
        ptV_ready = sem("ptV_ready")
        av_done = sem("av_done")
        upd_ready = sem("upd_ready")
        o_done = sem("o_done")
        x1_ready = sem("x1_ready")
        stats2 = sem("stats2")
        veps2 = sem("veps2")
        rstd2 = sem("rstd2")
        xn2_ready = sem("xn2_ready")
        x2t_done = sem("x2t_done")
        x2hi_ready = sem("x2hi_ready")
        x2_ready = sem("x2_ready")
        gate_done = sem("gate_done")
        up_done = sem("up_done")
        sil_ready = sem("sil_ready")
        g_ready = sem("g_ready")
        mid_done = sem("mid_done")
        gelu_ready = sem("gelu_ready")
        hi_ready = sem("hi_ready")
        h_ready = sem("h_ready")
        out_done = sem("out_done")
        y_ready = sem("y_ready")
        block_used = sem("block_used")
        scaled = [sem(f"scaled{j}") for j in range(2)]
        stored = [sem(f"stored{j}") for j in range(2)]
        block_loaded = [sem(f"block_loaded{j}") for j in range(2)]
        consts_ready = sem("consts_ready")
        wk_loaded = sem("wk_loaded")
        wq_loaded = sem("wq_loaded")
        wv_loaded = sem("wv_loaded")
        wo_loaded = sem("wo_loaded")
        bias_loaded = sem("bias_loaded")
        small_loaded = sem("small_loaded")
        chunk_cast = sem("chunk_cast")
        chunk_looked = sem("chunk_looked")
        counted = sem("counted")
        low_summed = sem("low_summed")
        flag_ready = sem("flag_ready")
        stats_seen = sem("stats_seen")
        chunk_loaded = [sem(f"chunk_loaded{i}") for i in range(len(landing))]

        def at(name, tile, k):
            value = tile * PER[name] + k
            return max(value, 0) if isinstance(value, int) else value

        chunks = ([(w1T, W1, k) for k in range(KD)] + [(w2T, W2, k) for k in range(KD)]
                  + [(h1T, H1, k) for k in range(KH)] + [(h2T, H2, k) for k in range(KH)]
                  + [(w3T, W3, 4 * k) for k in range(KH * D // CH)])
        assert len(chunks) == CHUNKS
        FIRST_BLOCKS = 3 * KH
        block = st.enter_context(nc.Block())

        @block.sync
        def _(sp):
            def load_tile(a):
                sp.wait_ge(xn_ready, at("xn_ready", a - 1, 2))
                sp.wait_ge(x_plus_b, at("x_plus_b", a - 1, 2))
                sp.dma_start(x_in[:], x[bass.ds(a, 1)].rearrange("o p n -> (o p) n")).then_inc(x_loaded, 16)
                sp.wait_ge(k_done, at("k_done", a - 1, 1))
                sp.wait_ge(v_done, at("v_done", a - 1, 2))
                sp.dma_start(cT[:], ctxT[bass.ds(a, 1)].rearrange("o p n -> (o p) n")).then_inc(ctx_loaded, 16)
                sp.wait_ge(kT_ready, at("kT_ready", a - 1, 2))
                sp.wait_ge(qT_ready, at("qT_ready", a - 1, 2))
                sp.wait_ge(mask_bias_ready, at("mask_bias_ready", a - 1, 1))
                sp.dma_start(mrow[:], mask_row[bass.ds(a, 1)].broadcast_to([P, T])).then_inc(mask_loaded, 16)
                sp.wait_ge(v_ready, at("v_ready", a - 1, 2))
                sp.dma_start(mcol[:], mask_col[bass.ds(a, 1)].rearrange("o p n -> (o p) n")).then_inc(mask_loaded, 16)

            def raw_block(f, n, src):
                sp.wait_ge(block_used, at("block_used", f, max(n - 1, 0)))
                dst = stage[n % 2][:].rearrange("p (k m) -> p k m", m=src.shape[2])[:, 0:src.shape[1], :]
                sp.dma_start(dst, src).then_inc(block_loaded[n % 2], 16)

            def first_blocks(f):
                for n in range(2 * KH):
                    src, p = (w1T, w2T)[n // 2 % 2], 2 * (n // 4) + n % 2
                    raw_block(f, n, src[:, :, p * P:(p + 1) * P])
                for m in range(KH):
                    raw_block(f, 2 * KH + m, h1T[:, :, m * P:(m + 1) * P])

            def last_blocks(f):
                for m in range(KH):
                    raw_block(f, 3 * KH + m, h2T[:, :, m * P:(m + 1) * P])
                for n in range(2):
                    raw_block(f, 4 * KH + n, w3T[:, 4 * n:4 * n + 4, :])

            def store(f):
                for j in range(NB):
                    sp.wait_ge(y_ready, at("y_ready", f, j + 1))
                    sp.dma_start(out[bass.ds(f * NB + j, 1)].rearrange("o p n -> (o p) n"),
                                 y[:, j, :]).then_inc(stored[j], 16)

            def tile(f, a, general, first=True):
                if general and first:
                    first_blocks(f)
                if a is not None:
                    load_tile(a)
                if general:
                    last_blocks(f)
                store(f)

            def tiles(general):
                tile(0, 2, general, first=False)
                with sp.Fori(1, TILES - 2) as i:
                    tile(i, i + 2, general)
                tile(TILES - 2, None, general)
                tile(TILES - 1, None, general)

            sp.dma_start(x_in[:], x[0]).then_inc(x_loaded, 16)
            sp.dma_start(cT[:], ctxT[0]).then_inc(ctx_loaded, 16)
            sp.dma_start(WK[:], wsT).then_inc(wk_loaded, 16)
            sp.dma_start(bcols[:], b_cols).then_inc(bias_loaded, 16)
            sp.dma_start(mrow[:], mask_row[0:1].broadcast_to([P, T])).then_inc(mask_loaded, 16)
            sp.dma_start(mcol[:], mask_col[0]).then_inc(mask_loaded, 16)
            sp.dma_start(WQ[:], wtT).then_inc(wq_loaded, 16)
            sp.dma_start(WV[:], wvT).then_inc(wv_loaded, 16)
            for dst, src in ((scols, s_cols), (bv_bc, b_v.broadcast_to([P, D])),
                             (bo_bc, b_out.broadcast_to([P, D])), (s3_bc, s3.broadcast_to([P, D]))):
                sp.dma_start(dst[:], src).then_inc(small_loaded, 16)
            for n, (src, _, k) in enumerate(chunks):
                if n == 2 * KD:
                    sp.dma_start(WO[:], woT).then_inc(wo_loaded, 16)
                if n == 2 * len(landing):
                    load_tile(1)
                if land[n] in land[:n]:
                    before = max(m for m in range(n) if land[m] == land[n])
                    sp.wait_ge(chunk_looked, before + 1)
                w = CH // src.shape[2]
                sp.dma_start(landing[land[n]].rearrange("p (k m) -> p k m", k=w), src[:, k:k + w, :])\
                    .then_inc(chunk_loaded[land[n]], 16)
            sp.wait_ge(flag_ready, 1)
            early_low_bits = sp.value_load(flag[0:1, 0:1], min_val=0, max_val=1)
            with sp.If(early_low_bits):
                first_blocks(0)
            with sp.Else():
                for j in range(2):
                    sp.sem_inc(block_loaded[j], 16 * FIRST_BLOCKS // 2)
            sp.wait_ge(flag_ready, 2)
            has_low_bits = sp.value_load(flag[0:1, 1:2], min_val=0, max_val=1)
            with sp.If(has_low_bits):
                tiles(True)
            with sp.Else():
                tiles(False)
            for j in range(NB):
                sp.wait_ge(stored[j], at("stored", TILES, 0))

        @block.tensor
        def _(pe):
            mm = nc.tensor.matmul

            def transposes_x(a):
                pe.wait_ge(xn_ready, at("xn_ready", a, 2))
                pe.wait_ge(x1_ready, at("x1_ready", a - 1, 2))
                for j in range(NB):
                    for c in range(KD):
                        ins = nc.tensor.transpose(G[0][:, c * T + j * P:c * T + (j + 1) * P],
                                                  xn[:, j, c * P:(c + 1) * P], ident[:])
                ins.then_inc(xt_done, 1)

            def project_k(a):
                pe.wait_ge(wk_loaded, 16)
                pe.wait_ge(ctx_loaded, at("ctx_loaded", a, 16))
                pe.wait_ge(x2_ready, at("x2_ready", a - 1, 2))
                for c in range(KD):
                    for k in range(KC):
                        ins = mm(G[1][:, c * T:(c + 1) * T], WK[:, k, c * P:(c + 1) * P], cT[:, k, :],
                                 start=k == 0, stop=k == KC - 1)
                ins.then_inc(k_done, 1)

            def project_q(a):
                pe.wait_ge(xnT_ready, at("xnT_ready", a, 1))
                pe.wait_ge(wq_loaded, 16)
                for c in range(KD):
                    for k in range(KD):
                        ins = mm(G[0][:, c * T:(c + 1) * T], WQ[:, k, c * P:(c + 1) * P], xnT[:, k, :],
                                 start=k == 0, stop=k == KD - 1)
                ins.then_inc(q_done, 1)

            def project_v(a, j):
                pe.wait_ge(wv_loaded, 16)
                pe.wait_ge(kT_ready, at("kT_ready", a, 2))
                for k in range(KC):
                    ins = mm(G[1][:, j * D:(j + 1) * D], cT[:, k, j * P:(j + 1) * P], WV[:, k, :],
                             start=k == 0, stop=k == KC - 1)
                ins.then_inc(v_done, 1)

            def scores(a, j):
                pe.wait_ge(kT_ready, at("kT_ready", a, 2))
                pe.wait_ge(qT_ready, at("qT_ready", a, 2))
                pe.wait_ge(masked, at("masked", a, 0 if j == 0 else 1))
                for c in range(KD):
                    for r in range(ROWS):
                        rows = slice(r * DH, (r + 1) * DH)
                        ins = mm(S[:, r, j, c, :], qT[rows, c, j * P:(j + 1) * P],
                                 kT[rows, c, j * P:(j + 1) * P], start=True, stop=True)
                ins.then_inc(scores_done, 1)

            def transpose_p(a, j):
                pe.wait_ge(probs_ready, at("probs_ready", a, j + 1))
                if j == 0:
                    pe.wait_ge(qT_ready, at("qT_ready", a, 2))
                    pe.wait_ge(vb_ready, at("vb_ready", a, 1))
                else:
                    pe.wait_ge(upd_ready, at("upd_ready", a, 1))
                    pe.wait_ge(ptV_ready, at("ptV_ready", a, 1))
                for c in range(KD):
                    for r in range(ROWS):
                        ins = nc.tensor.transpose(G[c][:, r * P:(r + 1) * P], pr[j][:, r, c, :], ident[:])
                    ins.then_inc(pt_done, 1)

            def attend(a, j):
                pe.wait_ge(v_ready, at("v_ready", a, 2))
                pe.wait_ge(ptA_ready, at("ptA_ready", a, j + 1))
                for c in range(KD):
                    if c == 1:
                        pe.wait_ge(ptV_ready, at("ptV_ready", a, j + 1))
                    for r in range(ROWS):
                        h = c * ROWS + r
                        ins = mm(G[0][r * DH:(r + 1) * DH, c * P:(c + 1) * P], v[:, j, h * DH:(h + 1) * DH],
                                 pT[:, c, r * P:(r + 1) * P], start=True, stop=True)
                ins.then_inc(av_done, 1)

            def out_proj(a, j):
                bank = G[1] if j == 0 else G[0]
                if j == 0:
                    pe.wait_ge(ptV_ready, at("ptV_ready", a, 2))
                pe.wait_ge(upd_ready, at("upd_ready", a, j + 1))
                pe.wait_ge(wo_loaded, 16)
                for k in range(2 * KD):
                    lhsT = xnT[:, k, j * P:(j + 1) * P] if k < KD else upd[:, k - KD, :]
                    ins = mm(bank[:, 0:D], lhsT, WO[:, k, :], start=k == 0, stop=k == 2 * KD - 1)
                ins.then_inc(o_done, 1)

            def transpose_x2(a, j):
                pe.wait_ge(xn2_ready, at("xn2_ready", a, j + 1))
                if j == 0:
                    pe.wait_ge(x1_ready, at("x1_ready", a, 1))
                else:
                    pe.wait_ge(x2_ready, at("x2_ready", a, 1))
                for c in range(KD):
                    ins = nc.tensor.transpose(G[1][:, c * P:(c + 1) * P], xn2[:, c * P:(c + 1) * P], ident[:])
                ins.then_inc(x2t_done, 1)

            def ffn_group(bank, W, cols, parts, general, f, n, ready=None):
                kk = W.shape[1]
                if general:
                    pe.wait_ge(block_loaded[n % 2], at("block_loaded", f, 16 * (n // 2 + 1)))
                    raw = stage[n % 2][:].rearrange("p (k m) -> p k m", m=P)
                for k in range(kk):
                    if ready is not None:
                        ready(k)
                    for q, part in enumerate(parts):
                        first, last = k == 0 and q == 0, k == kk - 1 and q == 1
                        if general:
                            ins = mm(bank, raw[:, k, :], part[:, k, :].bitcast(F32), start=first, stop=last)
                        else:
                            ins = mm(bank, W[:, k, cols], part[:, k, :], start=first, stop=last)
                if general:
                    ins.then_inc(block_used, 1)
                    pe.wait_ge(block_used, at("block_used", f, n + 1))
                    ins = pe.nop()
                return ins

            def gate_up(f, q, general):
                pe.wait_ge(x2_ready, at("x2_ready", f, 2))
                if q == 0:
                    pe.wait_ge(scaled[0], at("scaled", f - 1, 1))
                else:
                    pe.wait_ge(sil_ready, at("sil_ready", f, 2 * q))
                for h in range(2):
                    cols = slice((2 * q + h) * P, (2 * q + h + 1) * P)
                    ins = ffn_group(F[0][:, h, :], W1, cols, (x2h, x2l), general, f, 4 * q + h)
                ins.then_inc(gate_done, 1)
                if q == 0:
                    pe.wait_ge(scaled[1], at("scaled", f - 1, 1))
                else:
                    pe.wait_ge(g_ready, at("g_ready", f, 2 * q))
                for h in range(2):
                    cols = slice((2 * q + h) * P, (2 * q + h + 1) * P)
                    ins = ffn_group(F[1][:, h, :], W2, cols, (x2h, x2l), general, f, 4 * q + 2 + h)
                ins.then_inc(up_done, 1)

            def middle(f, q, half, general):
                W, parts = (H1, (hAh, hAl)) if q < 8 else (H2, (hBh, hBl))
                if half == 0 and q == 4:
                    pe.wait_ge(sil_ready, at("sil_ready", f, KH))
                elif half == 0 and q == 5:
                    pe.wait_ge(g_ready, at("g_ready", f, KH))
                elif half == 0:
                    pe.wait_ge(gelu_ready, at("gelu_ready", f, 2 * (q - 5)))
                m = 2 * (q % 4) + half

                def ready(k):
                    if m == 0 and k % 2 == 0:
                        pe.wait_ge(h_ready, at("h_ready", f, q - 4 + k // 2 + 1))

                ins = ffn_group(F[q % 2][:, half, :], W, slice(m * P, (m + 1) * P), parts, general, f,
                                2 * KH + (q // 4 - 1) * KH + m, ready)
                if half:
                    ins.then_inc(mid_done, 1)

            def ffn_out(f, general):
                if general:
                    for n in range(2):
                        pe.wait_ge(block_loaded[n], at("block_loaded", f, 16 * (2 * KH + 1)))
                for j, ks in ((0, range(6)), (1, range(6)), (0, (6, 7)), (1, (6, 7))):
                    if ks[0] == 0:
                        pe.wait_ge(gelu_ready, at("gelu_ready", f, 14 + 2 * j))
                    for k in ks:
                        if j == 0 and k % 2 == 0:
                            pe.wait_ge(h_ready, at("h_ready", f, 8 + k // 2 + 1))
                        for q, h in enumerate((hAh, hAl)):
                            first, last = k == 0 and q == 0, k == KH - 1 and q == 1
                            lhsT = h[:, k, j * P:(j + 1) * P]
                            if general:
                                raw = stage[k // 4][:, k % 4 * D:(k % 4 + 1) * D]
                                ins = mm(F[j][:, 0, :], lhsT.bitcast(F32), raw, start=first, stop=last)
                            else:
                                ins = mm(F[j][:, 0, :], lhsT, W3[:, k, :], start=first, stop=last)
                    if ks[-1] == KH - 1:
                        ins.then_inc(out_done, 1)
                if general:
                    pe.wait_ge(out_done, at("out_done", f, 2))
                    pe.sem_inc(block_used, 2)

            def first_part(f, a, general):
                attn, ffn = a is not None, f is not None
                if attn:
                    transposes_x(a)
                for q in range(4):
                    if ffn:
                        gate_up(f, q, general)
                    if attn and q == 0:
                        project_k(a)
                        project_q(a)
                    if attn and q == 1:
                        scores(a, 0)
                    if attn and q == 2:
                        scores(a, 1)
                    if attn and q == 3:
                        project_v(a, 0)
                        project_v(a, 1)
                for q in range(4, 8):
                    for half in range(2):
                        if attn and (q, half) == (6, 0):
                            transpose_p(a, 0)
                        if attn and (q, half) == (7, 0):
                            attend(a, 0)
                        if attn and (q, half) == (7, 1):
                            transpose_p(a, 1)
                        if ffn:
                            middle(f, q, half, general)

            def second_part(f, a, general):
                attn, ffn = a is not None, f is not None
                for q in range(8, 12):
                    for half in range(2):
                        if attn and (q, half) == (8, 0):
                            attend(a, 1)
                            out_proj(a, 0)
                        if attn and (q, half) == (9, 1):
                            out_proj(a, 1)
                        if attn and (q, half) == (10, 0):
                            transpose_x2(a, 0)
                        if attn and (q, half) == (11, 1):
                            transpose_x2(a, 1)
                        if ffn:
                            middle(f, q, half, general)
                if ffn:
                    ffn_out(f, general)

            def tiles(general):
                second_part(0, 1, general)
                with pe.Fori(1, TILES - 1) as i:
                    first_part(i, i + 1, general)
                    second_part(i, i + 1, general)
                first_part(TILES - 1, None, general)
                second_part(TILES - 1, None, general)

            pe.wait_ge(consts_ready, 3)
            first_part(None, 0, False)
            second_part(None, 0, False)
            pe.wait_ge(flag_ready, 1)
            early_low_bits = pe.value_load(flag[0:1, 0:1], min_val=0, max_val=1)
            with pe.If(early_low_bits):
                first_part(0, 1, True)
            with pe.Else():
                first_part(0, 1, False)
                pe.sem_inc(block_used, FIRST_BLOCKS)
            pe.wait_ge(flag_ready, 2)
            has_low_bits = pe.value_load(flag[0:1, 1:2], min_val=0, max_val=1)
            with pe.If(has_low_bits):
                tiles(True)
            with pe.Else():
                tiles(False)

        @block.scalar
        def _(act):
            fn = nc.scalar.activation

            def silu(f, q):
                act.wait_ge(gate_done, at("gate_done", f, q + 1))
                for p in (2 * q, 2 * q + 1):
                    act.wait_ge(g_ready, at("g_ready", f, max(p - 1, 0)))
                    fn(sil[:, p % 2, :], F[0][:, p % 2, :], ACT.Silu, scale=scols[:, p:p + 1]).then_inc(sil_ready, 1)

            def gelu(f, q):
                act.wait_ge(mid_done, at("mid_done", f, q - 3))
                act.wait_ge(h_ready, at("h_ready", f, q - 1))
                for m in (0, 1):
                    col = KH + 2 * q + m
                    fn(g[:, q % 2, m, :], F[q % 2][:, m, :], ACT.Gelu,
                       scale=scols[:, col:col + 1]).then_inc(gelu_ready, 1)

            def copy_xnT(a):
                act.wait_ge(xt_done, at("xt_done", a, 1))
                act.wait_ge(o_done, at("o_done", a - 1, 2))
                fn(xnT[:].rearrange("p c t -> p (c t)"), G[0][:], ACT.Copy).then_inc(xnT_ready, 1)

            def exps(a, j):
                act.wait_ge(negmax_ready, at("negmax_ready", a, j + 1))
                for r in range(ROWS):
                    for c in range(KD):
                        h = r * KD + c
                        ins = fn(pr[j][:, r, c, :], pr[j][:, r, c, :], ACT.Exp, bias=nmx[:, j, h:h + 1],
                                 scale=SCALE, accum_out=den[:, j, h:h + 1])
                ins.then_inc(exp_ready, 1)

            def scale_v(a):
                act.wait_ge(vb_ready, at("vb_ready", a, 1))
                act.wait_ge(mask_loaded, at("mask_loaded", a, 32))
                act.wait_ge(av_done, at("av_done", a - 1, 2))
                for j in range(NB):
                    fn(v[:, j, :], vb[:, j, :], ACT.Copy, scale=mcol[:, j:j + 1]).then_inc(v_ready, 1)

            def copy_pT(a, j):
                act.wait_ge(pt_done, at("pt_done", a, 2 * j + 1))
                act.wait_ge(av_done, at("av_done", a, j))
                fn(pT[:, 0, :], G[0][:], ACT.Copy).then_inc(ptA_ready, 1)

            def copy_upd(a, j):
                act.wait_ge(av_done, at("av_done", a, j + 1))
                act.wait_ge(o_done, at("o_done", a, j))
                fn(upd[:].rearrange("p c t -> p (c t)"), G[0][:, 0:KD * P], ACT.Copy).then_inc(upd_ready, 1)

            def x2_hi(a, j):
                act.wait_ge(x2t_done, at("x2t_done", a, j + 1))
                act.wait_ge(up_done, at("up_done", a - 1, 4))
                fn(x2h[:, :, j * P:(j + 1) * P], G[1][:, 0:KD * P].rearrange("p (c t) -> p c t", c=KD),
                   ACT.Copy).then_inc(x2hi_ready, 1)

            def tile(f, a, coming=range(0)):
                attn, ffn = a is not None, f is not None
                left = iter(coming)

                def casts(count):
                    for n in islice(left, count):
                        cast(n)

                if ffn:
                    casts(2)
                if attn:
                    copy_xnT(a)
                    casts(2 if ffn else 4)
                if ffn and coming:
                    act.wait_ge(chunk_looked, CHUNKS - 2)
                if ffn:
                    for q in range(4):
                        silu(f, q)
                        if q == 1:
                            casts(2)
                if attn:
                    exps(a, 0)
                    casts(1)
                    exps(a, 1)
                    casts(2)
                for q in range(4, 12):
                    if attn and q == 6:
                        scale_v(a)
                        copy_pT(a, 0)
                        casts(2)
                    if attn and q == 7:
                        copy_upd(a, 0)
                        casts(1)
                        copy_pT(a, 1)
                        casts(2)
                    if attn and q == 8:
                        copy_upd(a, 1)
                        casts(3)
                    if attn and q == 10:
                        x2_hi(a, 0)
                        casts(1)
                    if attn and q == 11:
                        x2_hi(a, 1)
                        casts(CHUNKS)
                    if ffn:
                        gelu(f, q)

            def cast(n):
                _, W, k = chunks[n]
                w = CH // W.shape[2]
                act.wait_ge(chunk_loaded[land[n]], landed(n))
                fn(W[:, k:k + w, :], landing[land[n]].rearrange("p (k m) -> p k m", k=w), ACT.Copy)\
                    .then_inc(chunk_cast, 1)

            act.wait_ge(small_loaded, 64)
            tile(None, 0, range(EARLY))
            tile(0, 1, range(EARLY, CHUNKS))
            with act.Fori(1, TILES - 1) as i:
                tile(i, i + 1)
            tile(TILES - 1, None)

        @block.vector
        def _(dve):
            V = nc.vector

            def keep_residual(f):
                dve.wait_ge(x1_ready, at("x1_ready", f, 2))
                dve.wait_ge(y_ready, at("y_ready", f - 1, 2))
                V.tensor_copy(res[:], x1[:]).then_inc(res_ready, 1)

            def ln1_stats(a):
                dve.wait_ge(x_loaded, at("x_loaded", a, 16))
                for j in range(NB):
                    V.bn_stats(st1[:, j, :], x_in[:, j, :]).then_inc(stats1, 1)
                dve.wait_ge(stats1, at("stats1", a, 2))
                dve.sem_inc(stats_seen, 1)
                for j in range(NB):
                    V.bn_aggr(mv1[:, j, :], st1[:, j, :]).then_inc(stats1, 1)
                dve.wait_ge(stats1, at("stats1", a, 4))
                V.tensor_scalar_add(ve1[:], mv1[:, :, 1], EPS).then_inc(veps1, 1)

            def mask_bias(a):
                dve.wait_ge(mask_loaded, at("mask_loaded", a, 32))
                V.tensor_scalar(mbias[:], mrow[:], 0.0, MASKED, ALU.is_equal, ALU.mult).then_inc(mask_bias_ready, 1)

            def ln1_apply(a):
                dve.wait_ge(rstd1, at("rstd1", a, 1))
                dve.wait_ge(xt_done, at("xt_done", a - 1, 1))
                for j in range(NB):
                    V.tensor_scalar(xn[:, j, :], x_in[:, j, :], mv1[:, j, 0:1], rs1[:, j:j + 1],
                                        ALU.subtract, ALU.mult).then_inc(xn_ready, 1)

            def bias_mask_k(a):
                dve.wait_ge(k_done, at("k_done", a, 1))
                dve.wait_ge(mask_loaded, at("mask_loaded", a, 32))
                dve.wait_ge(scores_done, at("scores_done", a - 1, 2))
                for c in range(KD):
                    V.scalar_tensor_tensor(kT[:, c, :], G[1][:, c * T:(c + 1) * T], bcols[:, c:c + 1],
                                           mrow[:], ALU.add, ALU.mult).then_inc(kT_ready, 1)

            def bias_mask_q(a):
                dve.wait_ge(q_done, at("q_done", a, 1))
                dve.wait_ge(mask_loaded, at("mask_loaded", a, 32))
                dve.wait_ge(scores_done, at("scores_done", a - 1, 2))
                for c in range(KD):
                    V.scalar_tensor_tensor(qT[:, c, :], G[0][:, c * T:(c + 1) * T], bcols[:, KD + c:KD + c + 1],
                                           mrow[:], ALU.add, ALU.mult).then_inc(qT_ready, 1)

            def bias_v(a):
                dve.wait_ge(v_done, at("v_done", a, 2))
                dve.wait_ge(v_ready, at("v_ready", a - 1, 2))
                dve.wait_ge(small_loaded, 64)
                V.tensor_tensor(vb[:], G[1][:].rearrange("p (j n) -> p j n", j=NB),
                                    bv_bc[:].unsqueeze(1).broadcast_to([P, NB, D]), ALU.add).then_inc(vb_ready, 1)

            def mask_scores(a, j):
                dve.wait_ge(scores_done, at("scores_done", a, j + 1))
                dve.wait_ge(pt_done, at("pt_done", a - 1, 2 * j + 2))
                dve.wait_ge(mask_bias_ready, at("mask_bias_ready", a, 1))
                bias = mbias[:, j * P:(j + 1) * P].unsqueeze(1).unsqueeze(1).broadcast_to([P, ROWS, KD, P])
                V.tensor_tensor(pr[j][:], S[:, :, j, :, :], bias, ALU.add).then_inc(masked, 1)

            def row_max(a, j):
                dve.wait_ge(masked, at("masked", a, j + 1))
                V.tensor_reduce(mx[:, j, :], pr[j][:].rearrange("p r c s -> p (r c) s"),
                                AX.X, ALU.max).then_inc(max_ready, 1)
                dve.wait_ge(max_ready, at("max_ready", a, j + 1))
                dve.wait_ge(exp_ready, at("exp_ready", a - 1, j + 1))
                V.tensor_scalar_mul(nmx[:, j, :], mx[:, j, :], -SCALE).then_inc(negmax_ready, 1)

            def normalise(a, j):
                dve.wait_ge(exp_ready, at("exp_ready", a, j + 1))
                V.reciprocal(rden[:, j, :], den[:, j, :]).then_inc(recip, 1)
                dve.wait_ge(recip, at("recip", a, j + 1))
                p8 = pr[j][:].rearrange("p r c s -> p (r c) s")
                V.tensor_tensor(p8, p8, rden[:, j, :].unsqueeze(2).broadcast_to([P, HEADS, P]),
                                ALU.mult).then_inc(probs_ready, 1)

            def copy_pT(a, j):
                dve.wait_ge(pt_done, at("pt_done", a, 2 * j + 2))
                dve.wait_ge(av_done, at("av_done", a, j))
                V.tensor_copy(pT[:, 1, :], G[1][:]).then_inc(ptV_ready, 1)

            def residual_ln2_stats(a, j):
                bank = G[1] if j == 0 else G[0]
                dve.wait_ge(o_done, at("o_done", a, j + 1))
                dve.wait_ge(x_plus_b, at("x_plus_b", a, j + 1))
                V.tensor_tensor(x1[:, j, :], bank[:, 0:D], x1[:, j, :], ALU.add).then_inc(x1_ready, 1)
                dve.wait_ge(x1_ready, at("x1_ready", a, j + 1))
                V.bn_stats(st2[:, j, :], x1[:, j, :]).then_inc(stats2, 1)
                dve.wait_ge(stats2, at("stats2", a, 2 * j + 1))
                dve.sem_inc(stats_seen, 1)
                V.bn_aggr(mv2[:, j, :], st2[:, j, :]).then_inc(stats2, 1)
                dve.wait_ge(stats2, at("stats2", a, 2 * j + 2))
                V.tensor_scalar_add(ve2[:, j:j + 1], mv2[:, j, 1:2], EPS).then_inc(veps2, 1)

            def ln2_apply(a, j):
                dve.wait_ge(rstd2, at("rstd2", a, j + 1))
                dve.wait_ge(x2t_done, at("x2t_done", a, j))
                V.tensor_scalar(xn2[:], x1[:, j, :], mv2[:, j, 0:1], rs2[:, j:j + 1],
                                    ALU.subtract, ALU.mult).then_inc(xn2_ready, 1)

            def x2_lo(a, j):
                dve.wait_ge(x2hi_ready, at("x2hi_ready", a, j + 1))
                dve.wait_ge(up_done, at("up_done", a - 1, 4))
                part = slice(j * P, (j + 1) * P)
                V.tensor_tensor(x2l[:, :, part], G[1][:, 0:KD * P].rearrange("p (c t) -> p c t", c=KD),
                                    x2h[:, :, part].bitcast(F32), ALU.subtract).then_inc(x2_ready, 1)

            def gate_times_up(f, q):
                dve.wait_ge(up_done, at("up_done", f, q + 1))
                dve.wait_ge(h_ready, at("h_ready", f, max(q - 1, 0)))
                for p in (2 * q, 2 * q + 1):
                    dve.wait_ge(sil_ready, at("sil_ready", f, p + 1))
                    V.scalar_tensor_tensor(g[:, q % 2, p % 2, :], F[1][:, p % 2, :], scols[:, KH + p:KH + p + 1],
                                               sil[:, p % 2, :], ALU.mult, ALU.mult).then_inc(g_ready, 1)

            def split(f, q):
                hi, lo = ((hAh, hAl), (hBh, hBl), (hAh, hAl))[q // 4]
                pair = slice(2 * (q % 4), 2 * (q % 4) + 2)
                if q < 4:
                    dve.wait_ge(g_ready, at("g_ready", f, 2 * q + 2))
                    dve.wait_ge(out_done, at("out_done", f - 1, 2))
                elif q < 8:
                    dve.wait_ge(gelu_ready, at("gelu_ready", f, 2 * (q - 4) + 2))
                    dve.wait_ge(mid_done, at("mid_done", f - 1, 8))
                else:
                    dve.wait_ge(gelu_ready, at("gelu_ready", f, 2 * (q - 4) + 2))
                    dve.wait_ge(mid_done, at("mid_done", f, 4))
                V.tensor_copy(hi[:, pair, :], g[:, q % 2, :, :]).then_inc(hi_ready, 1)
                dve.wait_ge(hi_ready, at("hi_ready", f, q + 1))
                V.tensor_tensor(lo[:, pair, :], g[:, q % 2, :, :], hi[:, pair, :].bitcast(F32),
                                ALU.subtract).then_inc(h_ready, 1)

            def scale_out(f, j):
                dve.wait_ge(out_done, at("out_done", f, j + 1))
                dve.wait_ge(stored[j], at("stored", f - 1, 16))
                V.tensor_tensor(y[:, j, :], F[j][:, 0, :], s3_bc[:], ALU.mult).then_inc(scaled[j], 1)

            def add_residual(f, j):
                dve.wait_ge(scaled[j], at("scaled", f, 1))
                V.tensor_tensor(y[:, j, :], y[:, j, :], res[:, j, :], ALU.add).then_inc(y_ready, 1)

            def tile(f, a, following, coming=range(0)):
                attn, ffn = a is not None, f is not None
                left = iter(coming)

                def looks(count):
                    for n in islice(left, count):
                        look(n)

                if ffn:
                    keep_residual(f)
                    looks(4)
                if attn:
                    mask_bias(a)
                for q in range(4):
                    if ffn:
                        gate_times_up(f, q)
                    if attn and q == 2:
                        row_max(a, 0)
                        if not ffn:
                            looks(2)
                    if ffn:
                        split(f, q)
                    if attn and q == 0:
                        bias_mask_k(a)
                        bias_mask_q(a)
                        if not ffn:
                            looks(2)
                    if attn and q in (1, 2):
                        mask_scores(a, q - 1)
                if attn:
                    row_max(a, 1)
                    normalise(a, 0)
                    bias_v(a)
                    looks(2)
                    if ffn and coming:
                        count_low_bits(1, CHUNKS)
                for q in range(4, 12):
                    if ffn and coming and q == 5:
                        raise_flag(1)
                    if attn and q == 6:
                        copy_pT(a, 0)
                        normalise(a, 1)
                        looks(2)
                    if attn and q == 7:
                        copy_pT(a, 1)
                        looks(4)
                    if attn and q == 8:
                        residual_ln2_stats(a, 0)
                        ln2_apply(a, 0)
                    if attn and q == 9:
                        residual_ln2_stats(a, 1)
                        looks(1)
                    if attn and q == 10:
                        x2_lo(a, 0)
                        ln2_apply(a, 1)
                        looks(2)
                    if attn and q == 11:
                        x2_lo(a, 1)
                        looks(3)
                    if ffn:
                        split(f, q)
                    if following is not None and q == 10:
                        ln1_stats(following)
                    if following is not None and q == 11:
                        ln1_apply(following)
                if attn:
                    looks(CHUNKS)
                if ffn:
                    scale_out(f, 0)
                    scale_out(f, 1)
                    add_residual(f, 0)
                    add_residual(f, 1)

            def count_low_bits(i, n):
                dve.wait_ge(chunk_looked, n)
                V.tensor_reduce(unequal_sum[:, i:i + 1], unequal[:, 0:n], AX.X, ALU.max).then_inc(counted, 1)

            def raise_flag(i):
                dve.wait_ge(low_summed, i + 1)
                V.tensor_scalar_min(flag[:, i:i + 1], most[:, i:i + 1], 1.0).then_inc(flag_ready, 1)

            def look(n):
                _, W, k = chunks[n]
                w = CH // W.shape[2]
                raw = landing[land[n]].rearrange("p (k m) -> p k m", k=w)
                dve.wait_ge(chunk_cast, n + 1)
                V.scalar_tensor_tensor(raw, raw, 1.0, W[:, k:k + w, :].bitcast(F32), ALU.mult, ALU.not_equal,
                                       accum_out=unequal[:, n:n + 1]).then_inc(chunk_looked, 1)

            ln1_stats(0)
            ln1_apply(0)
            dve.wait_ge(bias_loaded, 16)
            tile(None, 0, 1, range(EARLY))
            count_low_bits(0, EARLY)
            raise_flag(0)
            tile(0, 1, 2, range(EARLY, CHUNKS))
            with dve.Fori(1, TILES - 2) as i:
                tile(i, i + 1, i + 2)
            tile(TILES - 2, TILES - 1, None)
            tile(TILES - 1, None, None)

        @block.gpsimd
        def _(pool):
            Gp = nc.gpsimd

            def inverse_std1(a):
                pool.wait_ge(veps1, at("veps1", a, 1))
                Gp.tensor_tensor(rs1[:], ve1[:], neg_half[:], ALU.pow).then_inc(rstd1, 1)

            def add_bias(a):
                pool.wait_ge(x_loaded, at("x_loaded", a, 16))
                pool.wait_ge(res_ready, at("res_ready", a, 0))
                for j in range(NB):
                    Gp.tensor_tensor(x1[:, j, :], x_in[:, j, :], bo_bc[:], ALU.add).then_inc(x_plus_b, 1)

            def inverse_std2(a, j):
                pool.wait_ge(veps2, at("veps2", a, j + 1))
                Gp.tensor_tensor(rs2[:, j:j + 1], ve2[:, j:j + 1], neg_half[:, 0:1], ALU.pow).then_inc(rstd2, 1)

            def sum_low_bits(i):
                pool.wait_ge(counted, i + 1)
                Gp.tensor_reduce(most[:, i:i + 1], unequal_sum[:, i:i + 1], AX.C, ALU.max).then_inc(low_summed, 1)

            def tile(a, following, late_chunks=False):
                add_bias(a)
                if late_chunks:
                    sum_low_bits(1)
                for j in range(NB):
                    inverse_std2(a, j)
                if following is not None:
                    inverse_std1(following)

            pool.memset(ident[:], 0.0).then_inc(consts_ready, 1)
            pool.memset(neg_half[:], -0.5).then_inc(consts_ready, 1)
            pool.wait_ge(consts_ready, 2)
            pool.affine_select(out=ident[:], in_=ident[:], compare_op=ALU.not_equal, fill=1.0, base=0,
                               pattern=[[-1, P]], channel_multiplier=1).then_inc(consts_ready, 1)
            inverse_std1(0)
            pool.wait_ge(small_loaded, 64)
            tile(0, 1)
            sum_low_bits(0)
            tile(1, 2, late_chunks=True)
            with pool.Fori(2, TILES - 1) as a:
                tile(a, a + 1)
            tile(TILES - 1, None)


def kernel(x, ctx_2048, mask_BxS2_fk1, L0_xattn_W_src, L0_xattn_b_src, L0_xattn_W_tgt, L0_xattn_b_tgt,
           L0_xattn_W_out, L0_xattn_b_out, L0_ffn_w1_w, L0_ffn_w1_s, L0_ffn_w2_w, L0_ffn_w2_s, L0_ffn_h1_w,
           L0_ffn_h1_s, L0_ffn_h2_w, L0_ffn_h2_s, L0_ffn_w3_w, L0_ffn_w3_s):
    import concourse.bacc as bacc
    from concourse.bass_utils import run_bass_kernel_spmd

    A = np.asarray

    def by_chunk(w):
        w = A(w).T
        return w.reshape(w.shape[0] // P, P, w.shape[1]).transpose(1, 0, 2)

    def columns(*vs):
        return np.concatenate([A(v).reshape(-1, P).T for v in vs], axis=1)

    Ws, bs = A(L0_xattn_W_src), A(L0_xattn_b_src)
    m = A(mask_BxS2_fk1)
    arrays = {
        "x_t": A(x).reshape(TILES, NB, P, D).transpose(0, 2, 1, 3).reshape(TILES, P, NB * D),
        "ctx_t": A(ctx_2048).reshape(TILES, T, KC, P).transpose(0, 3, 2, 1).reshape(TILES, P, KC * T),
        "mask_row": m.reshape(TILES, T),
        "mask_col": m.reshape(TILES, NB, P).transpose(0, 2, 1),
        "wk": by_chunk(Ws[:D]), "wv": by_chunk(Ws[D:]), "wq": by_chunk(L0_xattn_W_tgt), "wo": by_chunk(L0_xattn_W_out),
        "b_kq": columns(bs[:D], L0_xattn_b_tgt), "b_v": bs[D:].reshape(1, D), "b_o": A(L0_xattn_b_out).reshape(1, D),
        "w1": by_chunk(L0_ffn_w1_w), "w2": by_chunk(L0_ffn_w2_w), "h1": by_chunk(L0_ffn_h1_w),
        "h2": by_chunk(L0_ffn_h2_w), "w3": by_chunk(L0_ffn_w3_w),
        "s_all": columns(L0_ffn_w1_s, L0_ffn_w2_s, L0_ffn_h1_s, L0_ffn_h2_s), "s_3": A(L0_ffn_w3_s).reshape(1, D),
    }
    arrays = {n: np.ascontiguousarray(a) for n, a in arrays.items()}
    nc = bacc.Bacc("TRN2", target_bir_lowering=False, num_devices=1)
    ins = [nc.dram_tensor(n, a.shape, mybir.dt.from_np(a.dtype), kind="ExternalInput").ap() for n, a in arrays.items()]
    out = nc.dram_tensor("out", (B, P, D), F32, kind="ExternalOutput").ap()
    program(nc, *ins, out)
    r = run_bass_kernel_spmd(nc, [arrays], core_ids=[0])
    return r.results[0]["out"]
```
